# Optimizing a Trainium2 kernel written in Bass

```python
import numpy as np
import jax
import jax.numpy as jnp

def _softmax(x, axis=-1):
    return jax.nn.softmax(x, axis=axis)

def _gelu(x):
    return jax.nn.gelu(x, approximate=True)

def _silu(x):
    return jax.nn.silu(x)

def _sigmoid(x):
    return jax.nn.sigmoid(x)

def _layernorm(x, axis=-1, eps=1e-05):
    m = jnp.mean(x, axis=axis, keepdims=True)
    v = jnp.var(x, axis=axis, keepdims=True)
    return (x - m) / jnp.sqrt(v + eps)

def _scatter_add(tgt, idx, src, axis=0):
    return tgt.at[idx].add(src)

def _segment_sum(src, seg, n):
    return jax.ops.segment_sum(src, seg, n)
kernel_name = 'mk_decoder_preln_d1_seqx_r8_b837f6'

def setup_inputs(seed: int=0):
    np.random.seed(seed)
    _w = jnp.asarray

    def _rec_inputs():
        import jax
        import jax.numpy as jnp
        _rk = jax.random.key(seed)
        x = 0.0003765 + 1 * jax.random.normal(jax.random.fold_in(_rk, 1), (16, 128, 256), jnp.float32)
        _lenS = 128 - jax.random.randint(jax.random.fold_in(_rk, 7), (16,), 0, max(1, 128 // 4) + 1, jnp.int32)
        _lenS2 = 128 - jax.random.randint(jax.random.fold_in(_rk, 8), (16,), 0, max(1, 128 // 4) + 1, jnp.int32)
        _ctx_2048P = jax.random.normal(jax.random.fold_in(_rk, 11), (16, 16, 256), jnp.float32)
        _ctx_2048c = jax.random.dirichlet(jax.random.fold_in(_rk, 511), 0.3 * jnp.ones((16,), jnp.float32), (16, 128))
        _ctx_2048t = jnp.einsum('bsk,bkd->bsd', _ctx_2048c, _ctx_2048P)
        _ctx_2048t = _ctx_2048t * jax.lax.rsqrt(jnp.mean(jnp.square(_ctx_2048t)) + 1e-12) * 0.953939
        ctx_2048 = -0.000292821 + 1.00034 * (_ctx_2048t + 0.3 * jax.random.normal(jax.random.fold_in(_rk, 611), (16, 128, 256), jnp.float32))
        return (x, ctx_2048)
    x, ctx_2048 = _rec_inputs()

    def _L0_attn_setup():
        import jax, jax.numpy as jnp
        import numpy as np
        B, S, H_DIM = (2, 256, 256)
        N_HEADS, D_HEAD = (16, 128)
        key = jax.random.key(seed)
        k1, k2, k3 = jax.random.split(key, 3)
        x = jax.random.normal(k1, (B, S, H_DIM), dtype=jnp.float32)
        w_qkv = jax.random.normal(k2, (H_DIM, 3 * N_HEADS * D_HEAD), dtype=jnp.float32) * 0.02
        w_o = jax.random.normal(k3, (N_HEADS * D_HEAD, H_DIM), dtype=jnp.float32) * 0.02
        return {'x': x, 'w_qkv': w_qkv, 'w_o': w_o}
    _L0_attn_all = _L0_attn_setup()
    _L0_attn_in = {k: v for k, v in _L0_attn_all.items() if k in ('w_qkv', 'w_o')}
    del _L0_attn_all

    def _L0_xattn_setup():
        import jax, jax.numpy as jnp
        import numpy as np
        key = jax.random.key(seed)
        k1, k2, k3, k4, k5 = jax.random.split(key, 5)
        B, D_MODEL, L = (2, 128, 256)
        HEAD_DIM = 8
        H = D_MODEL // HEAD_DIM
        return {'k': jax.random.normal(k1, (B, D_MODEL, L), dtype=jnp.float32), 'v': jax.random.normal(k2, (B, D_MODEL, L), dtype=jnp.float32), 'q': jax.random.normal(k3, (B, D_MODEL, L), dtype=jnp.float32), 'ssm_kernel': jax.random.normal(k4, (H, L), dtype=jnp.float32), 'D': jax.random.normal(k5, (H,), dtype=jnp.float32), 'head_dim': HEAD_DIM}
    _L0_xattn_all = _L0_xattn_setup()
    _L0_xattn_in = {k: v for k, v in _L0_xattn_all.items() if k in ('ssm_kernel', 'D')}
    del _L0_xattn_all

    def _L0_ffn_setup():
        import jax, jax.numpy as jnp
        import numpy as np

        def binarize_weight(w):
            alpha = jnp.mean(jnp.abs(w), axis=tuple(range(1, w.ndim)), keepdims=True)
            bw = jnp.where(w >= 0, 1.0, -1.0) * alpha
            return jax.lax.stop_gradient(bw - w) + w
        key = jax.random.key(seed)
        k1, k2, k3 = jax.random.split(key, 3)
        in_features, out_features = (256, 256)
        x = jax.random.normal(k1, (8, 256, in_features), dtype=jnp.float32)
        std = np.sqrt(2.0 / out_features).astype(np.float32)
        weight = jax.random.normal(k2, (out_features, in_features), dtype=jnp.float32) * std
        bias = jax.random.normal(k3, (out_features,), dtype=jnp.float32) * 0.01
        return {'x': x, 'weight': weight, 'bias': bias}
    _L0_ffn_all = _L0_ffn_setup()
    _L0_ffn_in = {k: v for k, v in _L0_ffn_all.items() if k in ('weight', 'bias')}
    del _L0_ffn_all
    return {'x': x, 'ctx_2048': ctx_2048, 'L0_attn_w_qkv': _L0_attn_in['w_qkv'], 'L0_attn_w_o': _L0_attn_in['w_o'], 'L0_xattn_ssm_kernel': _L0_xattn_in['ssm_kernel'], 'L0_xattn_D': _L0_xattn_in['D'], 'L0_ffn_weight': _L0_ffn_in['weight'], 'L0_ffn_bias': _L0_ffn_in['bias']}

def reference(x, ctx_2048, L0_attn_w_qkv, L0_attn_w_o, L0_xattn_ssm_kernel, L0_xattn_D, L0_ffn_weight, L0_ffn_bias):
    import jax
    import jax.numpy as jnp

    def _L0_attn_ref(x, w_qkv, w_o):
        import jax, jax.numpy as jnp
        import numpy as np
        B, S, H_DIM = (2, 256, 256)
        N_HEADS, D_HEAD = (16, 128)
        b, s, _ = x.shape
        qkv = jnp.einsum('bsh,hf->bsf', x, w_qkv)
        qkv = qkv.reshape(b, s, 3, N_HEADS, D_HEAD)
        q, k, v = (qkv[:, :, 0], qkv[:, :, 1], qkv[:, :, 2])
        q = q.transpose(0, 2, 1, 3)
        k = k.transpose(0, 2, 1, 3)
        v = v.transpose(0, 2, 1, 3)
        scores = jnp.einsum('bhqd,bhkd->bhqk', q, k) / jnp.sqrt(jnp.float32(D_HEAD))
        probs = jax.nn.softmax(scores, axis=-1)
        values = jnp.einsum('bhqk,bhkd->bhkd', probs, v)
        values = values.transpose(0, 2, 1, 3).reshape(b, s, N_HEADS * D_HEAD)
        out = jnp.einsum('bsf,fh->bsh', values, w_o)
        return out

    def _L0_xattn_ref(k, v, q, ssm_kernel, D, head_dim):
        import jax, jax.numpy as jnp
        import numpy as np
        B, HD, L = k.shape
        H = HD // head_dim
        fft_size = 2 * L
        k_ = k.reshape(B, H, head_dim, L)
        v_ = v.reshape(B, H, head_dim, L)
        q_ = q.reshape(B, H, head_dim, L)
        kv = jnp.einsum('bhil,bhjl->bijhl', k_, v_)
        kv_f = jnp.fft.rfft(kv, n=fft_size)
        kernel_f = jnp.fft.rfft(ssm_kernel, n=fft_size)
        y = jnp.fft.irfft(kv_f * kernel_f, n=fft_size)[..., :L]
        out = y + kv * D[None, None, None, :, None]
        out = jnp.einsum('bijhl,bhil->bjhl', out, q_)
        out = jnp.transpose(out, (0, 2, 1, 3)).reshape(B, H * head_dim, L)
        return out.astype(k.dtype)

    def _L0_ffn_ref(x, weight, bias):
        import jax, jax.numpy as jnp
        import numpy as np

        def binarize_weight(w):
            alpha = jnp.mean(jnp.abs(w), axis=tuple(range(1, w.ndim)), keepdims=True)
            bw = jnp.where(w >= 0, 1.0, -1.0) * alpha
            return jax.lax.stop_gradient(bw - w) + w
        bw = binarize_weight(weight)
        return jnp.einsum('bsi,oi->bso', x, bw) + bias
    x = x + _L0_attn_ref(_layernorm(x, axis=-1), L0_attn_w_qkv, L0_attn_w_o)
    x = x + _L0_xattn_ref(ctx_2048, ctx_2048, _layernorm(x, axis=-1), L0_xattn_ssm_kernel, L0_xattn_D, 8)
    x = x + _L0_ffn_ref(_layernorm(x, axis=-1), L0_ffn_weight, L0_ffn_bias)
    return x

_drawn_inputs = setup_inputs


def setup_inputs(seed=0):
    import zlib

    import numpy as np

    out = dict(_drawn_inputs(seed))
    spreads = {}
    factors = {'L0_ffn_bias': 200.0}
    for name, (base, spread) in spreads.items():
        noise = np.random.default_rng([zlib.crc32(name.encode()), seed]).standard_normal(out[name].shape)
        drawn = base * np.exp(spread * noise) if base else spread * noise
        out[name] = jnp.asarray(drawn.astype(out[name].dtype))
    for name, factor in factors.items():
        out[name] = (out[name] * factor).astype(out[name].dtype)
    return out
```

```python
import concourse.bass as bass
from concourse import mybir
from contextlib import ExitStack

F32 = mybir.dt.float32
FR = mybir.dt.float32r
ALU = mybir.AluOpType
ACT = mybir.ActivationFunctionType
AX = mybir.AxisListType


def decoder_layer(nc, x, ctx_in, w_qkv, w_o, ssm, skip, w_lin, bias, out):
    P = 128
    NSEQ, SEQ, DM = x.shape
    HD = P
    HEADS = w_o.shape[0] // HD
    PAIRS = HEADS // 2
    KC = DM // P
    NB = 4
    GROUPS = NSEQ // NB
    TOK = NB * SEQ
    SCALE = float(HD) ** -0.5
    EPS = 1e-5
    CH = ssm.shape[0]
    CI = P // CH
    TRI = CI * (CI + 1) // 2
    OFF = [i * CI - i * (i - 1) // 2 for i in range(CI)]
    QH = CH // 4
    STEPS = HEADS + 4

    ctx = ExitStack()
    with ctx:
        def sb(name, shape, dt=F32):
            return ctx.enter_context(nc.sbuf_tensor(name, [P] + shape, dt))

        def bank(name):
            return ctx.enter_context(nc.psum_tensor(name, [P, 512], F32))

        def sem(name):
            return ctx.enter_context(nc.semaphore(name))

        ident = sb("ident", [P])
        zeros = sb("zeros", [KC * 2 * P])
        minus_half = sb("minus_half", [NB])
        toeplitz = sb("toeplitz", [CH, 2 * P])
        m_hi = sb("m_hi", [KC, PAIRS, 2 * DM], FR)
        m_lo = sb("m_lo", [KC, PAIRS, 2 * DM], FR)
        lin_T = sb("lin_T", [KC, DM])
        bias_sb = sb("bias_sb", [DM])
        w_raw = sb("w_raw", [2, 2, KC, HD])
        w_hi = sb("w_hi", [2, 2, KC, HD], FR)
        w_lo = sb("w_lo", [2, 2, KC, HD], FR)
        x_in = sb("x_in", [NB, DM])
        ln1 = sb("ln1", [NB, DM])
        xT_hi = sb("xT_hi", [KC, TOK], FR)
        xT_lo = sb("xT_lo", [KC, TOK], FR)
        qk_hi = sb("qk_hi", [2, 2, TOK], FR)
        qk_lo = sb("qk_lo", [2, 2, TOK], FR)
        probs = sb("probs", [2, NB, SEQ])
        neg_max = sb("neg_max", [HEADS, NB])
        row_sum = sb("row_sum", [HEADS, NB])
        row_inv = sb("row_inv", [HEADS, NB])
        col_sum = sb("col_sum", [HEADS, NB])
        acc = sb("acc", [NB, DM])
        ctx_sb = sb("ctx_sb", [NB, DM])
        ctx_T = sb("ctx_T", [KC, CH, NB, CI])
        kv = sb("kv", [2, KC, QH, NB, TRI])
        x2 = sb("x2", [NB, DM])
        ln23 = sb("ln23", [NB, DM])
        tailT = sb("tailT", [KC * TOK])
        ln2_T = tailT[:, :].rearrange("p (c h b i) -> p c h b i", c=KC, h=CH, b=NB)
        ln3_T = tailT[:, :].rearrange("p (c t) -> p c t", c=KC)
        conv = sb("conv", [KC, CH, NB, TRI])
        gated = sb("gated", [KC, QH * NB, CI, CI])
        mixT = sb("mixT", [KC, NB, CH, CI])
        y = sb("y", [NB, DM])
        stats = sb("stats", [3, NB, 6])
        mv = sb("mv", [3, NB, 2])
        veps = sb("veps", [3, NB])
        rstd = sb("rstd", [3, NB])
        pace = sb("pace", [4])
        flat = conv[:, :, :, :].rearrange("p c h b t -> p (c h b t)")
        WB = KC * 2 * HD
        wv_sb = flat[:, 0:2 * WB].rearrange("p (r c n) -> p r c n", r=2, c=KC)
        wo_sb = flat[:, 2 * WB:4 * WB].rearrange("p (r h n) -> p r h n", r=2, h=2)
        wv_T = flat[:, 4 * WB:6 * WB].rearrange("p (r h n) -> p r h n", r=2, h=2)
        lin_sb = flat[:, 6 * WB:7 * WB].rearrange("p (o n) -> p o n", o=KC)
        lin_bin = flat[:, 7 * WB:8 * WB].rearrange("p (o n) -> p o n", o=KC)
        alpha = sb("alpha", [KC])
        pad_sb = sb("pad_sb", [P + 2 * P])
        skip_sb = sb("skip_sb", [1])
        pad_dram = nc.dram_tensor("padded_kernel", [CH, 3 * P], F32, kind="Internal")
        rows_dram = nc.dram_tensor("toeplitz_rows", [P, CH, 2 * P], F32, kind="Internal")

        bank_q, bank_k, bank_s, bank_c = bank("bank_q"), bank("bank_k"), bank("bank_s"), bank("bank_c")
        bank_u = [bank("bank_u0"), bank("bank_u1")]
        bank_x = [bank("bank_x0"), bank("bank_x1")]

        x_loaded, ctx_loaded = sem("x_loaded"), sem("ctx_loaded")
        w_loaded = [sem("w_loaded0"), sem("w_loaded1")]
        prep_loaded = [sem("prep_loaded0"), sem("prep_loaded1")]
        rows_stored = sem("rows_stored")
        lin_loaded, ssm_loaded, pad_stored, toeplitz_loaded = (sem("lin_loaded"), sem("ssm_loaded"),
                                                               sem("pad_stored"), sem("toeplitz_loaded"))
        y_free = sem("y_free")
        ln_stats = [sem(f"ln_stats{k}") for k in range(3)]
        ln_mv = [sem(f"ln_mv{k}") for k in range(3)]
        ln_var = [sem(f"ln_var{k}") for k in range(3)]
        ln_rstd = [sem(f"ln_rstd{k}") for k in range(3)]
        ln_ready = [sem(f"ln_ready{k}") for k in range(3)]
        xT_done, xT_hi_ready, xT_ready = sem("xT_done"), sem("xT_hi_ready"), sem("xT_ready")
        w_hi_ready, w_ready = sem("w_hi_ready"), sem("w_ready")
        qk_done = [sem("q_done"), sem("k_done")]
        qk_hi_ready = [sem("q_hi_ready"), sem("k_hi_ready")]
        qk_ready = [sem("q_ready"), sem("k_ready")]
        scores_done, max_ready, probs_ready = sem("scores_done"), sem("max_ready"), sem("probs_ready")
        inv_ready, col_done, col_ready = sem("inv_ready"), sem("col_done"), sem("col_ready")
        u_done, u_added = sem("u_done"), sem("u_added")
        ctxT_done, ctxT_saved, kv_ready = sem("ctxT_done"), sem("ctxT_saved"), sem("kv_ready")
        conv_done, conv_saved = sem("conv_done"), sem("conv_saved")
        ln2T_done, ln2T_saved = sem("ln2T_done"), sem("ln2T_saved")
        gated_ready, mix_ready = sem("gated_ready"), sem("mix_ready")
        back_done, x3_ready = sem("back_done"), sem("x3_ready")
        ln3T_done, ln3T_saved = sem("ln3T_done"), sem("ln3T_saved")
        y_biased, lin_done, y_ready = sem("y_biased"), sem("lin_done"), sem("y_ready")
        consts_ready, pad_zeroed, pad_ready = sem("consts_ready"), sem("pad_zeroed"), sem("pad_ready")
        lin_step, lin_ready, linT_done, linT_saved = (sem("lin_step"), sem("lin_ready"), sem("linT_done"),
                                                      sem("linT_saved"))
        wvT_done, wvT_saved = sem("wvT_done"), sem("wvT_saved")
        m_done, m_hi_ready, m_ready = sem("m_done"), sem("m_hi_ready"), sem("m_ready")

        def after(eng, signal, count):
            if not isinstance(count, int) or count > 0:
                eng.wait_ge(signal, count)

        x_dram = x.rearrange("(g b) s d -> g s b d", b=NB)
        ctx_dram = ctx_in.rearrange("(g b) s d -> g s b d", b=NB)
        out_dram = out.rearrange("(g b) s d -> g s b d", b=NB)
        w_dram = w_qkv.rearrange("(c p) (m n) -> m p c n", p=P, m=3)
        wo_dram = w_o.rearrange("(h d) n -> d h n", d=HD)
        lin_dram = w_lin.rearrange("(o p) n -> p o n", p=P)

        block = ctx.enter_context(nc.Block())

        @block.sync
        def _(sp):
            def load_head(g, h):
                after(sp, w_ready, g * HEADS + h - 1)
                for m in range(2):
                    sp.dma_start(w_raw[:, h % 2, m], w_dram[m, :, :, h * HD:(h + 1) * HD]).then_inc(w_loaded[h % 2], 16)

            def load_prep(p):
                after(sp, m_done, 2 * (p - 1))
                sp.dma_start(wv_sb[:, p % 2], w_dram[2, :, :, 2 * p * HD:(2 * p + 2) * HD]).then_inc(prep_loaded[p % 2], 16)
                sp.dma_start(wo_sb[:, p % 2], wo_dram[:, 2 * p:2 * p + 2, :]).then_inc(prep_loaded[p % 2], 16)

            def store_y(p):
                sp.wait_ge(y_ready, 2 * p + 2)
                sp.dma_start(out_dram[p], y[:, :, :]).then_inc(y_free, 16)

            sp.dma_start(x_in[:, :, :], x_dram[0]).then_inc(x_loaded, 16)
            load_head(0, 0)
            sp.dma_start(pad_sb[0:CH, P:3 * P], ssm).then_inc(ssm_loaded, 16)
            sp.dma_start(skip_sb[0:CH, :], skip.rearrange("(h a) -> h a", a=1)).then_inc(ssm_loaded, 16)
            load_head(0, 1)
            load_prep(0)
            sp.dma_start(lin_sb, lin_dram).then_inc(lin_loaded, 16)
            load_prep(1)
            sp.dma_start(ctx_sb[:, :, :], ctx_dram[0]).then_inc(ctx_loaded, 16)
            sp.dma_start(bias_sb[:, :], bias.rearrange("(a n) -> a n", a=1).partition_broadcast(P)).then_inc(y_free, 16)
            sp.wait_ge(pad_ready, 1)
            sp.dma_start(pad_dram[:, :], pad_sb[0:CH, :]).then_inc(pad_stored, 16)
            sp.wait_ge(pad_stored, 16)
            sp.dma_start(rows_dram[:, :, :].rearrange("l h m -> h l m"),
                         bass.AP(pad_dram, P, [[3 * P, CH], [-1, P], [1, 2 * P]])).then_inc(rows_stored, 16)
            sp.wait_ge(rows_stored, 16)
            sp.dma_start(toeplitz[:, :, :], rows_dram[:, :, :]).then_inc(toeplitz_loaded, 16)

            def next_inputs(g):
                sp.wait_ge(u_added, (g - 1) * 4 * HEADS + 2 * 4)
                sp.dma_start(x_in[:, :, :], x_dram[g]).then_inc(x_loaded, 16)

            def group(g, first):
                for h in range(2 if first else 0, HEADS):
                    load_head(g, h)
                    if first and h % 2 == 1 and h // 2 + 1 < PAIRS:
                        load_prep(h // 2 + 1)

            group(0, True)
            with sp.Fori(1, GROUPS) as g:
                next_inputs(g)
                group(g, False)
                store_y(g - 1)
                sp.wait_ge(ctxT_done, 2 * g)
                sp.dma_start(ctx_sb[:, :, :], ctx_dram[g]).then_inc(ctx_loaded, 16)
            store_y(GROUPS - 1)
            sp.wait_ge(y_free, 16 * (GROUPS + 1))

        @block.gpsimd
        def _(pool):
            def split_head(g, h):
                r = h % 2
                after(pool, qk_done[1], g * HEADS + h - 1)
                pool.wait_ge(w_loaded[r], g * 16 * HEADS + 32 * (h // 2 + 1))
                raw = w_raw[:, r].rearrange("p m c n -> p (m c n)")
                hi = w_hi[:, r].rearrange("p m c n -> p (m c n)")
                lo = w_lo[:, r].rearrange("p m c n -> p (m c n)")
                nc.gpsimd.tensor_tensor(hi, raw, zeros[:, :], ALU.add).then_inc(w_hi_ready, 1)
                pool.wait_ge(w_hi_ready, g * HEADS + h + 1)
                nc.gpsimd.tensor_tensor(lo, raw, hi.bitcast(F32), ALU.subtract).then_inc(w_ready, 1)

            def power(k, n):
                pool.wait_ge(ln_var[k], n + 1)
                nc.gpsimd.tensor_tensor(rstd[:, k], veps[:, k], minus_half[:, :], ALU.pow).then_inc(ln_rstd[k], 1)

            def products(g, q):
                if q == 0:
                    pool.wait_ge(ctxT_saved, 2 * g + 2)
                after(pool, conv_done, g * CH + QH * (q - 1))
                for i in range(CI):
                    k_i = ctx_T[:, :, q * QH:(q + 1) * QH, :, i:i + 1].rearrange("p c h b i -> p c (h b) i")
                    k_j = ctx_T[:, :, q * QH:(q + 1) * QH, :, i:CI].rearrange("p c h b i -> p c (h b) i")
                    o = kv[:, q % 2, :, :, :, OFF[i]:OFF[i] + CI - i].rearrange("p c h b t -> p c (h b) t")
                    last = nc.gpsimd.tensor_tensor(o, k_i.to_broadcast([P, KC, QH * NB, CI - i]), k_j, ALU.mult)
                last.then_inc(kv_ready, 1)

            def add_bias(p):
                pool.wait_ge(y_free, 16 * (p + 1))
                pool.wait_ge(x3_ready, 2 * p + 2)
                nc.gpsimd.tensor_tensor(y[:, :, :], x2[:, :, :],
                                        bias_sb[:, :].rearrange("p (b n) -> p b n", b=1).to_broadcast([P, NB, DM]),
                                        ALU.add).then_inc(y_biased, 1)

            nc.gpsimd.memset(zeros[:, :], 0.0)
            nc.gpsimd.memset(minus_half[:, :], -0.5).then_inc(consts_ready, 1)
            nc.gpsimd.memset(pad_sb[0:CH, 0:P], 0.0).then_inc(pad_zeroed, 1)
            nc.gpsimd.memset(ident[:, :], 0.0).then_inc(consts_ready, 1)
            pool.wait_ge(consts_ready, 2)
            nc.gpsimd.affine_select(out=ident[:, :], in_=ident[:, :], compare_op=ALU.not_equal, fill=1.0,
                                    base=0, pattern=[[-1, P]], channel_multiplier=1).then_inc(consts_ready, 1)

            def group(g, first):
                split_head(g, 0) if first else None
                power(0, g)
                if not first:
                    products(g - 1, 2)
                    split_head(g, 0)
                    products(g - 1, 3)
                for t in range(1, HEADS):
                    split_head(g, t)
                    if not first and t == 4:
                        power(1, g - 1)
                    if not first and t == 13:
                        power(2, g - 1)
                        add_bias(g - 1)
                for q in range(2):
                    products(g, q)

            group(0, True)
            with pool.Fori(1, GROUPS) as g:
                group(g, False)
            products(GROUPS - 1, 2)
            products(GROUPS - 1, 3)
            power(1, GROUPS - 1)
            power(2, GROUPS - 1)
            add_bias(GROUPS - 1)

        @block.scalar
        def _(act):
            def xT_high(g):
                for c in range(KC):
                    act.wait_ge(xT_done, 2 * g + c + 1)
                    after(act, u_done, g * 4 * PAIRS)
                    nc.scalar.activation(xT_hi[:, c], bank_x[c][:, :], ACT.Copy).then_inc(xT_hi_ready, 1)

            def qk_high(g, h, m):
                act.wait_ge(qk_done[m], g * HEADS + h + 1)
                after(act, scores_done, g * HEADS + h - 1)
                nc.scalar.activation(qk_hi[:, m, h % 2], (bank_q, bank_k)[m][:, :], ACT.Copy,
                                     scale=(SCALE, 1.0)[m]).then_inc(qk_hi_ready[m], 1)

            def exps(g, h):
                act.wait_ge(max_ready, g * HEADS + h + 1)
                after(act, col_done, g * HEADS + h - 1)
                for b in range(NB):
                    last = nc.scalar.activation(probs[:, h % 2, b], bank_s[:, b * SEQ:(b + 1) * SEQ], ACT.Exp,
                                                bias=neg_max[:, h, b:b + 1], accum_out=row_sum[:, h, b:b + 1])
                last.then_inc(probs_ready, 1)

            def save_ctxT(g):
                for c in range(KC):
                    act.wait_ge(ctxT_done, 2 * g + c + 1)
                    after(act, kv_ready, 4 * g)
                    nc.scalar.activation(ctx_T[:, c].rearrange("p h b i -> p b h i"),
                                         bank_x[c][:, :].rearrange("p (b h i) -> p b h i", b=NB, h=CH),
                                         ACT.Copy).then_inc(ctxT_saved, 1)

            def save_conv(p, h):
                act.wait_ge(conv_done, p * CH + h + 1)
                nc.scalar.activation(conv[:, :, h].rearrange("p c b t -> p c (b t)"),
                                     bank_x[h % 2][:, 0:KC * NB * TRI].rearrange("p (c n) -> p c n", c=KC),
                                     ACT.Copy).then_inc(conv_saved, 1)

            def save_ln2T(p):
                for c in range(KC):
                    act.wait_ge(ln2T_done, 2 * p + c + 1)
                    nc.scalar.activation(ln2_T[:, c].rearrange("p h b i -> p b h i"),
                                         bank_x[c][:, :].rearrange("p (b h i) -> p b h i", b=NB, h=CH),
                                         ACT.Copy).then_inc(ln2T_saved, 1)

            def save_ln3T(p):
                for c in range(KC):
                    act.wait_ge(ln3T_done, 2 * p + c + 1)
                    nc.scalar.activation(ln3_T[:, c], bank_x[c][:, :], ACT.Copy).then_inc(ln3T_saved, 1)

            def save_wvT(p):
                act.wait_ge(wvT_done, p + 1)
                nc.scalar.activation(wv_T[:, p % 2].rearrange("p h n -> p (h n)"), bank_x[0][:, :],
                                     ACT.Copy).then_inc(wvT_saved, 1)

            def m_high(p):
                for c in range(KC):
                    act.wait_ge(m_done, 2 * p + c + 1)
                    nc.scalar.activation(m_hi[:, c, p], bank_x[1 - c][:, :], ACT.Copy).then_inc(m_hi_ready, 1)

            def save_linT():
                act.wait_ge(linT_done, 1)
                nc.scalar.activation(lin_T[:, :, :].rearrange("p c n -> p (c n)"), bank_x[0][:, :],
                                     ACT.Copy).then_inc(linT_saved, 1)

            def group(g, first):
                if not first:
                    for h in range(8):
                        save_conv(g - 1, h)
                xT_high(g)
                if not first:
                    for h in range(8, 12):
                        save_conv(g - 1, h)
                for t in range(STEPS):
                    if t < HEADS:
                        qk_high(g, t, 0)
                        qk_high(g, t, 1)
                    if 1 <= t <= HEADS:
                        exps(g, t - 1)
                    if first:
                        if t < HEADS and t % 2 == 0:
                            save_wvT(t // 2)
                        if t < HEADS and t % 2 == 1:
                            m_high(t // 2)
                        if t == 16:
                            save_linT()
                    else:
                        if t < 4:
                            save_conv(g - 1, 12 + t)
                        if t == 4:
                            save_ln2T(g - 1)
                        if t == 14:
                            save_ln3T(g - 1)
                    if t == 17:
                        save_ctxT(g)

            group(0, True)
            with act.Fori(1, GROUPS) as g:
                group(g, False)
            for h in range(CH):
                save_conv(GROUPS - 1, h)
            save_ln2T(GROUPS - 1)
            save_ln3T(GROUPS - 1)

        @block.vector
        def _(dve):
            def ln_moments(k, n, src):
                for b in range(NB):
                    last = nc.vector.bn_stats(stats[:, k, b], src[:, b])
                last.then_inc(ln_stats[k], 1)
                dve.wait_ge(ln_stats[k], n + 1)
                nc.vector.tensor_copy(pace[:, 0:1], stats[:, k, 0, 0:1])
                for b in range(NB):
                    last = nc.vector.bn_aggr(mv[:, k, b], stats[:, k, b])
                last.then_inc(ln_mv[k], 1)
                dve.wait_ge(ln_mv[k], n + 1)
                nc.vector.tensor_scalar(veps[:, k], mv[:, k, :, 1], EPS, None, ALU.add).then_inc(ln_var[k], 1)

            def ln_normalise(k, n, src, dst):
                dve.wait_ge(ln_rstd[k], n + 1)
                for b in range(NB):
                    last = nc.vector.tensor_scalar(dst[:, b], src[:, b], mv[:, k, b, 0:1], rstd[:, k, b:b + 1],
                                                   ALU.subtract, ALU.mult)
                last.then_inc(ln_ready[k], 1)

            def xT_low(g):
                for c in range(KC):
                    dve.wait_ge(xT_hi_ready, 2 * g + c + 1)
                    nc.vector.tensor_tensor(xT_lo[:, c], bank_x[c][:, :], xT_hi[:, c].bitcast(F32),
                                            ALU.subtract).then_inc(xT_ready, 1)

            def qk_low(g, h, m):
                dve.wait_ge(qk_hi_ready[m], g * HEADS + h + 1)
                nc.vector.scalar_tensor_tensor(out=qk_lo[:, m, h % 2], in0=(bank_q, bank_k)[m][:, :],
                                               scalar=(SCALE, 1.0)[m], in1=qk_hi[:, m, h % 2].bitcast(F32),
                                               op0=ALU.mult, op1=ALU.subtract).then_inc(qk_ready[m], 1)

            def row_max(g, h):
                dve.wait_ge(scores_done, g * HEADS + h + 1)
                nc.vector.tensor_reduce(out=neg_max[:, h], in_=bank_s[:, :].rearrange("p (b k) -> p b k", b=NB),
                                        op=ALU.max, axis=AX.X, negate=True).then_inc(max_ready, 1)

            def row_inverse(g, h):
                dve.wait_ge(probs_ready, g * HEADS + h + 1)
                nc.vector.reciprocal(row_inv[:, h], row_sum[:, h]).then_inc(inv_ready, 1)

            def save_col(g, h):
                dve.wait_ge(col_done, g * HEADS + h + 1)
                nc.vector.tensor_copy(col_sum[:, h], bank_c[:, 0:NB]).then_inc(col_ready, 1)

            def add_u(g, p, b):
                n = g * 4 * PAIRS + NB * p + b
                dve.wait_ge(u_done, n + 1)
                dve.wait_ge(col_ready, g * HEADS + 2 * p + 2)
                for j in range(2):
                    h = 2 * p + j
                    if j == 1:
                        dve.wait_ge(u_added, 2 * n + 1)
                    nc.vector.scalar_tensor_tensor(
                        out=(x2 if h == HEADS - 1 else acc)[:, b], in0=bank_u[b % 2][:, j * DM:(j + 1) * DM],
                        scalar=col_sum[:, h, b:b + 1], in1=(x_in if h == 0 else acc)[:, b],
                        op0=ALU.mult, op1=ALU.add).then_inc(u_added, 1)

            def gate(p, q):
                hs = slice(q * QH, (q + 1) * QH)
                pc = conv[:, :, hs].rearrange("p c h b t -> p c (h b) t")
                qc = ln2_T[:, :, hs].rearrange("p c h b i -> p c (h b) i")
                if q == 0:
                    dve.wait_ge(ln2T_saved, 2 * p + 2)
                else:
                    dve.wait_ge(mix_ready, 4 * p + q)
                dve.wait_ge(conv_saved, p * CH + QH * (q + 1))
                for i in range(CI):
                    nc.vector.tensor_tensor(gated[:, :, :, i:CI, i], pc[:, :, :, OFF[i]:OFF[i] + CI - i],
                                            qc[:, :, :, i:i + 1].to_broadcast([P, KC, QH * NB, CI - i]), ALU.mult)
                for i in range(CI - 1):
                    last = nc.vector.tensor_tensor(gated[:, :, :, i, i + 1:CI], pc[:, :, :, OFF[i] + 1:OFF[i] + CI - i],
                                                   qc[:, :, :, i + 1:CI], ALU.mult)
                last.then_inc(gated_ready, 1)

            def mix(p, q):
                dve.wait_ge(gated_ready, 4 * p + q + 1)
                for c in range(KC):
                    last = nc.vector.tensor_reduce(
                        out=mixT[:, c, :, q * QH:(q + 1) * QH].rearrange("p b h j -> p h b j"),
                        in_=gated[:, c].rearrange("p (h b) j i -> p h b j i", h=QH), op=ALU.add, axis=AX.X)
                last.then_inc(mix_ready, 1)

            def add_mix(p):
                for s in range(2):
                    dve.wait_ge(back_done, 2 * p + s + 1)
                    t = x2[:, 2 * s:2 * s + 2].rearrange("p b n -> p (b n)")
                    nc.vector.tensor_tensor(t, bank_x[s][:, :], t, ALU.add).then_inc(x3_ready, 1)

            def add_lin(p):
                dve.wait_ge(y_biased, p + 1)
                for s in range(2):
                    dve.wait_ge(lin_done, 2 * p + s + 1)
                    t = y[:, 2 * s:2 * s + 2].rearrange("p b n -> p (b n)")
                    nc.vector.tensor_tensor(t, bank_x[s][:, :], t, ALU.add).then_inc(y_ready, 1)

            def m_low(p):
                for c in range(KC):
                    dve.wait_ge(m_hi_ready, 2 * p + c + 1)
                    nc.vector.tensor_tensor(m_lo[:, c, p], bank_x[1 - c][:, :], m_hi[:, c, p].bitcast(F32),
                                            ALU.subtract).then_inc(m_ready, 1)

            def binarise():
                dve.wait_ge(lin_loaded, 16)
                nc.vector.tensor_reduce(out=alpha[:, :], in_=lin_sb, op=ALU.add, axis=AX.X,
                                        apply_absolute_value=True).then_inc(lin_step, 1)
                nc.vector.tensor_scalar(lin_bin, lin_sb, 0.0, 2.0, ALU.is_ge, ALU.mult).then_inc(lin_step, 1)
                dve.wait_ge(lin_step, 2)
                nc.vector.tensor_scalar(alpha[:, :], alpha[:, :], 1.0 / DM, None, ALU.mult).then_inc(lin_step, 1)
                dve.wait_ge(lin_step, 3)
                for o in range(KC):
                    nc.vector.tensor_scalar(lin_bin[:, o], lin_bin[:, o], -1.0, alpha[:, o:o + 1],
                                            ALU.add, ALU.mult).then_inc(lin_step, 1)
                dve.wait_ge(lin_step, 5)
                nc.vector.tensor_tensor(lin_bin, lin_bin, lin_sb, ALU.subtract).then_inc(lin_step, 1)
                dve.wait_ge(lin_step, 6)
                nc.vector.tensor_tensor(lin_bin, lin_bin, lin_sb, ALU.add).then_inc(lin_ready, 1)

            def group(g, first):
                dve.wait_ge(x_loaded, 16 * g + 16)
                ln_moments(0, g, x_in)
                ln_normalise(0, g, x_in, ln1)
                if first:
                    dve.wait_ge(ssm_loaded, 32)
                    dve.wait_ge(pad_zeroed, 1)
                    nc.vector.tensor_tensor(pad_sb[0:CH, P:P + 1], pad_sb[0:CH, P:P + 1], skip_sb[0:CH, :],
                                            ALU.add).then_inc(pad_ready, 1)
                xT_low(g)
                for t in range(STEPS):
                    if t < HEADS:
                        qk_low(g, t, 0)
                        qk_low(g, t, 1)
                    if 1 <= t <= HEADS:
                        row_max(g, t - 1)
                    if t >= 4:
                        add_u(g, (t - 4) // 2, 2 * (t % 2))
                    if 1 <= t <= HEADS:
                        row_inverse(g, t - 1)
                    if 2 <= t <= HEADS + 1:
                        save_col(g, t - 2)
                    if t >= 4:
                        add_u(g, (t - 4) // 2, 2 * (t % 2) + 1)
                    if first:
                        if t < HEADS and t % 2 == 1:
                            m_low(t // 2)
                        if t == 12:
                            binarise()
                    else:
                        if t == 0:
                            dve.wait_ge(u_added, g * 8 * PAIRS)
                            ln_moments(1, g - 1, x2)
                        if t == 1:
                            ln_normalise(1, g - 1, x2, ln23)
                        if 5 <= t <= 8:
                            gate(g - 1, t - 5)
                            mix(g - 1, t - 5)
                        if t == 10:
                            add_mix(g - 1)
                        if t == 11:
                            dve.wait_ge(x3_ready, 2 * g)
                            ln_moments(2, g - 1, x2)
                        if t == 12:
                            ln_normalise(2, g - 1, x2, ln23)
                        if t == 15:
                            add_lin(g - 1)

            group(0, True)
            with dve.Fori(1, GROUPS) as g:
                group(g, False)
            p = GROUPS - 1
            dve.wait_ge(u_added, GROUPS * 8 * PAIRS)
            ln_moments(1, p, x2)
            ln_normalise(1, p, x2, ln23)
            for q in range(4):
                gate(p, q)
                mix(p, q)
            add_mix(p)
            dve.wait_ge(x3_ready, 2 * GROUPS)
            ln_moments(2, p, x2)
            ln_normalise(2, p, x2, ln23)
            add_lin(p)

        @block.tensor
        def _(pe):
            def three(out_, a_hi, a_lo, b_hi, b_lo, start, stop):
                nc.tensor.matmul(out_, a_hi, b_hi, start=start, stop=False)
                nc.tensor.matmul(out_, a_hi, b_lo, start=False, stop=False)
                return nc.tensor.matmul(out_, a_lo, b_hi, start=False, stop=stop)

            def transpose_tiles(src, done):
                for c in range(KC):
                    for b in range(NB):
                        last = nc.tensor.transpose(bank_x[c][:, b * P:(b + 1) * P], src[:, b, c * P:(c + 1) * P],
                                                   ident[:, :])
                    last.then_inc(done, 1)

            def project(g, h, m):
                if m == 0:
                    pe.wait_ge(w_ready, g * HEADS + h + 1)
                after(pe, qk_ready[m], g * HEADS + h)
                for c in range(KC):
                    last = three((bank_q, bank_k)[m][:, :], w_hi[:, h % 2, m, c], w_lo[:, h % 2, m, c],
                                 xT_hi[:, c], xT_lo[:, c], c == 0, c == KC - 1)
                last.then_inc(qk_done[m], 1)

            def scores(g, h):
                pe.wait_ge(qk_ready[0], g * HEADS + h + 1)
                pe.wait_ge(qk_ready[1], g * HEADS + h + 1)
                after(pe, probs_ready, g * HEADS + h)
                r = h % 2
                for b in range(NB):
                    s = slice(b * SEQ, (b + 1) * SEQ)
                    last = three(bank_s[:, s], qk_hi[:, 0, r, s], qk_lo[:, 0, r, s], qk_hi[:, 1, r, s],
                                 qk_lo[:, 1, r, s], True, True)
                last.then_inc(scores_done, 1)

            def column_sums(g, h):
                pe.wait_ge(inv_ready, g * HEADS + h + 1)
                after(pe, col_ready, g * HEADS + h)
                for b in range(NB):
                    last = nc.tensor.matmul(bank_c[:, b:b + 1], probs[:, h % 2, b], row_inv[:, h, b:b + 1],
                                            start=True, stop=True)
                last.then_inc(col_done, 1)

            def values(g, p, b):
                n = g * 4 * PAIRS + NB * p + b
                after(pe, u_added, 2 * n - 2)
                s = slice(b * P, (b + 1) * P)
                for c in range(KC):
                    last = three(bank_u[b % 2][:, :], xT_hi[:, c, s], xT_lo[:, c, s], m_hi[:, c, p], m_lo[:, c, p],
                                 c == 0, c == KC - 1)
                last.then_inc(u_done, 1)

            def convolve(p, h):
                if h % QH == 0:
                    pe.wait_ge(kv_ready, 4 * p + h // QH + 1)
                if h >= 2:
                    pe.wait_ge(conv_saved, p * CH + h - 1)
                src = kv[:, (h // QH) % 2, :, h % QH].rearrange("p c b t -> p c (b t)")
                n = NB * TRI
                near, far = toeplitz[:, h, 0:P], toeplitz[:, h, P:2 * P]
                o = bank_x[h % 2]
                nc.tensor.matmul(o[:, 0:n], near, src[:, 0], start=True, stop=True)
                nc.tensor.matmul(o[:, n:2 * n], far, src[:, 0], start=True, stop=False)
                nc.tensor.matmul(o[:, n:2 * n], near, src[:, 1], start=False, stop=True).then_inc(conv_done, 1)

            def transpose_ln2(p):
                pe.wait_ge(ln_ready[1], p + 1)
                pe.wait_ge(conv_saved, p * CH + CH)
                transpose_tiles(ln23, ln2T_done)

            def transpose_back(p):
                pe.wait_ge(mix_ready, 4 * p + 4)
                pe.wait_ge(ln2T_saved, 2 * p + 2)
                for s in range(2):
                    for b in range(2 * s, 2 * s + 2):
                        for c in range(KC):
                            last = nc.tensor.transpose(bank_x[s][:, (b % 2) * DM + c * P:(b % 2) * DM + (c + 1) * P],
                                                       mixT[:, c, b].rearrange("p h j -> p (h j)"), ident[:, :])
                    last.then_inc(back_done, 1)

            def transpose_ln3(p):
                pe.wait_ge(ln_ready[2], p + 1)
                transpose_tiles(ln23, ln3T_done)

            def linear(p):
                pe.wait_ge(ln3T_saved, 2 * p + 2)
                for s in range(2):
                    for b in range(2 * s, 2 * s + 2):
                        for c in range(KC):
                            last = nc.tensor.matmul(bank_x[s][:, (b % 2) * DM:(b % 2 + 1) * DM],
                                                    ln3_T[:, c, b * P:(b + 1) * P], lin_T[:, c],
                                                    start=c == 0, stop=c == KC - 1)
                    last.then_inc(lin_done, 1)

            def transpose_wv(p):
                pe.wait_ge(prep_loaded[p % 2], 32 * (p // 2 + 1))
                pe.wait_ge(*((m_ready, 2 * p) if p else (xT_ready, 2)))
                for j in range(2):
                    for c in range(KC):
                        last = nc.tensor.transpose(bank_x[0][:, (2 * j + c) * P:(2 * j + c + 1) * P],
                                                   wv_sb[:, p % 2, c, j * HD:(j + 1) * HD], ident[:, :])
                last.then_inc(wvT_done, 1)

            def multiply_wv_wo(p):
                pe.wait_ge(wvT_saved, p + 1)
                for c in range(KC):
                    for j in range(2):
                        last = nc.tensor.matmul(bank_x[1 - c][:, j * DM:(j + 1) * DM], wv_T[:, p % 2, j, c * P:(c + 1) * P],
                                                wo_sb[:, p % 2, j], start=True, stop=True)
                    last.then_inc(m_done, 1)

            def transpose_lin():
                pe.wait_ge(lin_ready, 1)
                pe.wait_ge(m_ready, 2 * PAIRS)
                for c in range(KC):
                    for o in range(KC):
                        last = nc.tensor.transpose(bank_x[0][:, (2 * c + o) * P:(2 * c + o + 1) * P],
                                                   lin_bin[:, o, c * P:(c + 1) * P], ident[:, :])
                last.then_inc(linT_done, 1)

            def group(g, first):
                if not first:
                    pe.wait_ge(ctxT_saved, 2 * g)
                    for h in range(8):
                        convolve(g - 1, h)
                    pe.wait_ge(conv_saved, (g - 1) * CH + 8)
                pe.wait_ge(ln_ready[0], g + 1)
                transpose_tiles(ln1, xT_done)
                if not first:
                    pe.wait_ge(xT_ready, 2 * g + 2)
                    for h in range(8, 12):
                        convolve(g - 1, h)
                pe.wait_ge(xT_ready, 2 * g + 2)
                for t in range(STEPS):
                    if t < HEADS:
                        project(g, t, 0)
                        project(g, t, 1)
                    if 1 <= t <= HEADS:
                        scores(g, t - 1)
                    if t >= 4:
                        if first and t % 2 == 0:
                            pe.wait_ge(m_ready, 2 * ((t - 4) // 2) + 2)
                        values(g, (t - 4) // 2, 2 * (t % 2))
                    if 2 <= t <= HEADS + 1:
                        column_sums(g, t - 2)
                    if t >= 4:
                        values(g, (t - 4) // 2, 2 * (t % 2) + 1)
                    if first:
                        if t < HEADS and t % 2 == 0:
                            transpose_wv(t // 2)
                        if t < HEADS and t % 2 == 1:
                            multiply_wv_wo(t // 2)
                        if t == 16:
                            transpose_lin()
                    else:
                        if t < 4:
                            convolve(g - 1, 12 + t)
                        if t == 3:
                            transpose_ln2(g - 1)
                        if t == 9:
                            transpose_back(g - 1)
                        if t == 13:
                            transpose_ln3(g - 1)
                        if t == 14:
                            linear(g - 1)
                    if t == 16:
                        if first:
                            pe.wait_ge(linT_saved, 1)
                        else:
                            pe.wait_ge(y_ready, 2 * g)
                        pe.wait_ge(ctx_loaded, 16 * g + 16)
                        transpose_tiles(ctx_sb, ctxT_done)

            pe.wait_ge(consts_ready, 3)
            group(0, True)
            pe.wait_ge(toeplitz_loaded, 16)
            with pe.Fori(1, GROUPS) as g:
                group(g, False)
            p = GROUPS - 1
            pe.wait_ge(ctxT_saved, 2 * GROUPS)
            for h in range(CH):
                convolve(p, h)
            transpose_ln2(p)
            transpose_back(p)
            transpose_ln3(p)
            linear(p)


_INS = ["x", "ctx_2048", "L0_attn_w_qkv", "L0_attn_w_o", "L0_xattn_ssm_kernel", "L0_xattn_D", "L0_ffn_weight",
        "L0_ffn_bias"]


def kernel(**inputs):
    import numpy as _np
    import concourse.bacc as _bacc
    from concourse import mybir as _mybir
    from concourse.bass_utils import run_bass_kernel_spmd as _run

    nc = _bacc.Bacc("TRN2", target_bir_lowering=False, num_devices=1)
    arrays, args = {}, []
    for name in _INS:
        a = _np.ascontiguousarray(inputs[name])
        arrays[f"in_{name}"] = a
        args.append(nc.dram_tensor(f"in_{name}", a.shape, _mybir.dt.from_np(a.dtype), kind="ExternalInput").ap())
    args.append(nc.dram_tensor("out_0", inputs["x"].shape, _mybir.dt.float32, kind="ExternalOutput").ap())
    decoder_layer(nc, *args)
    r = _run(nc, [arrays], core_ids=[0])
    return r.results[0]["out_0"]
```

```python
import concourse.bass as bass
from concourse import mybir
from contextlib import ExitStack

F32 = mybir.dt.float32
FR = mybir.dt.float32r
ALU = mybir.AluOpType
ACT = mybir.ActivationFunctionType
AX = mybir.AxisListType


def decoder_layer(nc, x, ctx_in, w_qkv, w_o, ssm, skip, w_lin, bias, out):
    P = 128
    NSEQ, SEQ, DM = x.shape
    HD = P
    HEADS = w_o.shape[0] // HD
    PAIRS = HEADS // 2
    KC = DM // P
    NB = 4
    GROUPS = NSEQ // NB
    LAST = GROUPS - 1
    TOK = NB * SEQ
    SCALE = float(HD) ** -0.5
    EPS = 1e-5
    CH = ssm.shape[0]
    CI = P // CH
    TRI = CI * (CI + 1) // 2
    OFF = [i * CI - i * (i - 1) // 2 for i in range(CI)]
    QH = CH // 4
    STEPS = HEADS + 4
    MIXING_AT = {2: [("gate", 0, 0), ("gate", 0, 1)], 3: [("gate", 0, 2), ("mix", 0, 0)], 4: [("mix", 0, 1)],
                 5: [("mix", 1, 0), ("mix", 1, 1)], 6: [("gate", 2, 0), ("gate", 2, 1)],
                 7: [("gate", 2, 2), ("mix", 2, 0)], 8: [("mix", 2, 1)], 10: [("mix", 3, 0), ("mix", 3, 1)]}
    CONV_AT = {16: range(0, 3), 17: range(3, 6), 18: range(6, 9), 19: range(9, 12), STEPS: range(12, CH)}

    ctx = ExitStack()
    with ctx:
        def sb(name, shape, dt=F32):
            return ctx.enter_context(nc.sbuf_tensor(name, [P] + shape, dt))

        def bank(name):
            return ctx.enter_context(nc.psum_tensor(name, [P, 512], F32))

        def sem(name):
            return ctx.enter_context(nc.semaphore(name))

        ident = sb("ident", [P])
        zeros = sb("zeros", [KC * 2 * P])
        minus_half = sb("minus_half", [NB])
        toeplitz = sb("toeplitz", [CH, 2 * P])
        m_hi = sb("m_hi", [KC, PAIRS, 2 * DM], FR)
        m_lo = sb("m_lo", [KC, PAIRS, 2 * DM], FR)
        lin_T = sb("lin_T", [KC, DM])
        bias_sb = sb("bias_sb", [DM])
        w_raw = sb("w_raw", [2, 2, KC, HD])
        w_hi = sb("w_hi", [2, 2, KC, HD], FR)
        w_lo = sb("w_lo", [2, 2, KC, HD], FR)
        x_in = sb("x_in", [NB, DM])
        ln1 = sb("ln1", [NB, DM])
        xT_hi = sb("xT_hi", [KC, TOK], FR)
        xT_lo = sb("xT_lo", [KC, TOK], FR)
        qk = sb("qk", [2, 2, TOK])
        probs = sb("probs", [2, NB, SEQ])
        neg_max = sb("neg_max", [HEADS, NB])
        row_sum = sb("row_sum", [HEADS, NB])
        row_inv = sb("row_inv", [HEADS, NB])
        col_sum = sb("col_sum", [HEADS, NB])
        acc = sb("acc", [NB, DM])
        ctx_sb = sb("ctx_sb", [NB, DM])
        ctx_T = sb("ctx_T", [KC, CH, NB, CI])
        kv = sb("kv", [2, KC, QH, NB, TRI])
        x2 = sb("x2", [NB, DM])
        ln23 = sb("ln23", [NB, DM])
        tailT = sb("tailT", [KC * TOK])
        ln2_T = tailT[:, :].rearrange("p (c h b i) -> p c h b i", c=KC, h=CH, b=NB)
        ln3_T = tailT[:, :].rearrange("p (c t) -> p c t", c=KC)
        conv = sb("conv", [KC, CH, NB, TRI])
        gated = [sb("gated0", [KC, QH * NB, CI, CI]), sb("gated1", [KC, QH * NB, CI, CI])]
        mixT = sb("mixT", [KC, NB, CH, CI])
        y = sb("y", [NB, DM])
        stats = sb("stats", [3, NB, 6])
        mv = sb("mv", [3, NB, 2])
        veps = sb("veps", [3, NB])
        rstd = sb("rstd", [3, NB])
        pace = sb("pace", [4])
        flat = conv[:, :, :, :].rearrange("p c h b t -> p (c h b t)")
        WB = KC * 2 * HD
        wv_sb = flat[:, 0:2 * WB].rearrange("p (r c n) -> p r c n", r=2, c=KC)
        wo_sb = flat[:, 2 * WB:4 * WB].rearrange("p (r h n) -> p r h n", r=2, h=2)
        wv_T = flat[:, 4 * WB:6 * WB].rearrange("p (r h n) -> p r h n", r=2, h=2)
        lin_sb = flat[:, 6 * WB:7 * WB].rearrange("p (o n) -> p o n", o=KC)
        lin_bin = flat[:, 7 * WB:8 * WB].rearrange("p (o n) -> p o n", o=KC)
        alpha = sb("alpha", [KC])
        pad_sb = sb("pad_sb", [P + 2 * P])
        skip_sb = sb("skip_sb", [1])
        pad_dram = nc.dram_tensor("padded_kernel", [CH, 3 * P], F32, kind="Internal")
        rows_dram = nc.dram_tensor("toeplitz_rows", [P, CH, 2 * P], F32, kind="Internal")

        bank_q, bank_k, bank_s, bank_c = bank("bank_q"), bank("bank_k"), bank("bank_s"), bank("bank_c")
        bank_u = [bank("bank_u0"), bank("bank_u1")]
        bank_x = [bank("bank_x0"), bank("bank_x1")]

        x_loaded, ctx_loaded = sem("x_loaded"), sem("ctx_loaded")
        w_loaded = [sem("w_loaded0"), sem("w_loaded1")]
        prep_loaded = [sem("prep_loaded0"), sem("prep_loaded1")]
        rows_stored = sem("rows_stored")
        lin_loaded, ssm_loaded, pad_stored, toeplitz_loaded = (sem("lin_loaded"), sem("ssm_loaded"),
                                                               sem("pad_stored"), sem("toeplitz_loaded"))
        y_free = sem("y_free")
        ln_stats = [sem(f"ln_stats{k}") for k in range(3)]
        ln_mv = [sem(f"ln_mv{k}") for k in range(3)]
        ln_var = [sem(f"ln_var{k}") for k in range(3)]
        ln_rstd = [sem(f"ln_rstd{k}") for k in range(3)]
        ln_ready = [sem(f"ln_ready{k}") for k in range(3)]
        xT_done, xT_hi_ready, xT_ready = sem("xT_done"), sem("xT_hi_ready"), sem("xT_ready")
        w_hi_ready, w_ready = sem("w_hi_ready"), sem("w_ready")
        qk_done = [sem("q_done"), sem("k_done")]
        qk_ready = [sem("q_ready"), sem("k_ready")]
        scores_done, max_ready, probs_ready = sem("scores_done"), sem("max_ready"), sem("probs_ready")
        inv_ready, col_done, col_ready = sem("inv_ready"), sem("col_done"), sem("col_ready")
        u_done, u_added = sem("u_done"), sem("u_added")
        ctxT_done, ctxT_saved, kv_ready = sem("ctxT_done"), sem("ctxT_saved"), sem("kv_ready")
        conv_done, conv_saved = sem("conv_done"), sem("conv_saved")
        ln2T_done, ln2T_saved = sem("ln2T_done"), sem("ln2T_saved")
        gated_ready, mix_ready = [sem("gated_ready0"), sem("gated_ready1")], sem("mix_ready")
        back_done, x3_ready = sem("back_done"), sem("x3_ready")
        ln3T_done, ln3T_saved = sem("ln3T_done"), sem("ln3T_saved")
        y_biased, lin_done, y_ready = sem("y_biased"), sem("lin_done"), sem("y_ready")
        consts_ready, pad_zeroed, pad_ready = sem("consts_ready"), sem("pad_zeroed"), sem("pad_ready")
        lin_step, lin_ready, linT_done, linT_saved = (sem("lin_step"), sem("lin_ready"), sem("linT_done"),
                                                      sem("linT_saved"))
        wvT_done, wvT_saved = sem("wvT_done"), sem("wvT_saved")
        m_done, m_hi_ready, m_ready = sem("m_done"), sem("m_hi_ready"), sem("m_ready")

        def after(eng, signal, count):
            if not isinstance(count, int) or count > 0:
                eng.wait_ge(signal, count)

        def gate_part(eng, q, part):
            hs = slice(q * QH, (q + 1) * QH)
            pc = conv[:, :, hs].rearrange("p c h b t -> p c (h b) t")
            qc = ln2_T[:, :, hs].rearrange("p c h b i -> p c (h b) i")
            o = gated[q % 2]
            if part < 2:
                for i in (range(3), range(3, CI))[part]:
                    last = eng.tensor_tensor(o[:, :, :, i:CI, i], pc[:, :, :, OFF[i]:OFF[i] + CI - i],
                                             qc[:, :, :, i:i + 1].to_broadcast([P, KC, QH * NB, CI - i]), ALU.mult)
            else:
                for j in range(CI - 1):
                    last = eng.tensor_tensor(o[:, :, :, j, j + 1:CI], pc[:, :, :, OFF[j] + 1:OFF[j] + CI - j],
                                             qc[:, :, :, j + 1:CI], ALU.mult)
            return last

        x_dram = x.rearrange("(g b) s d -> g s b d", b=NB)
        ctx_dram = ctx_in.rearrange("(g b) s d -> g s b d", b=NB)
        out_dram = out.rearrange("(g b) s d -> g s b d", b=NB)
        w_dram = w_qkv.rearrange("(c p) (m n) -> m p c n", p=P, m=3)
        wo_dram = w_o.rearrange("(h d) n -> d h n", d=HD)
        lin_dram = w_lin.rearrange("(o p) n -> p o n", p=P)

        block = ctx.enter_context(nc.Block())

        @block.sync
        def _(sp):
            def load_head(g, h):
                after(sp, w_ready, g * HEADS + h - 1)
                for m in range(2):
                    sp.dma_start(w_raw[:, h % 2, m], w_dram[m, :, :, h * HD:(h + 1) * HD]).then_inc(w_loaded[h % 2], 16)

            def load_prep(p):
                after(sp, m_done, 2 * (p - 1))
                sp.dma_start(wv_sb[:, p % 2], w_dram[2, :, :, 2 * p * HD:(2 * p + 2) * HD]).then_inc(prep_loaded[p % 2], 16)
                sp.dma_start(wo_sb[:, p % 2], wo_dram[:, 2 * p:2 * p + 2, :]).then_inc(prep_loaded[p % 2], 16)

            def store_y(p):
                for s in range(2):
                    sp.wait_ge(y_ready, 2 * p + s + 1)
                    sp.dma_start(out_dram[p, :, 2 * s:2 * s + 2], y[:, 2 * s:2 * s + 2]).then_inc(y_free, 16)

            def toeplitz_part(n):
                if n == 0:
                    sp.wait_ge(pad_ready, 1)
                    sp.dma_start(pad_dram[:, :], pad_sb[0:CH, :]).then_inc(pad_stored, 16)
                elif n == 1:
                    sp.wait_ge(pad_stored, 16)
                    sp.dma_start(rows_dram[:, :, :].rearrange("l h m -> h l m"),
                                 bass.AP(pad_dram, P, [[3 * P, CH], [-1, P], [1, 2 * P]])).then_inc(rows_stored, 16)
                else:
                    sp.wait_ge(rows_stored, 16)
                    sp.dma_start(toeplitz[:, :, :], rows_dram[:, :, :]).then_inc(toeplitz_loaded, 16)

            def group(g, first, last):
                for h in range(2, HEADS):
                    load_head(g, h)
                    if first and h % 2 == 1 and h // 2 + 1 < PAIRS:
                        load_prep(h // 2 + 1)
                    if first and h in (4, 6, 8):
                        toeplitz_part(h // 2 - 2)
                    if h == 6 and not last:
                        sp.wait_ge(ctxT_done, 2 * g + 2)
                        sp.dma_start(ctx_sb[:, :, :], ctx_dram[g + 1]).then_inc(ctx_loaded, 16)
                    if h == 9 and not last:
                        sp.wait_ge(u_added, g * 4 * HEADS + 2 * 4)
                        sp.dma_start(x_in[:, :, :], x_dram[g + 1]).then_inc(x_loaded, 16)
                if not last:
                    load_head(g + 1, 0)
                    load_head(g + 1, 1)
                if not first:
                    store_y(g - 1)

            sp.dma_start(x_in[:, :, :], x_dram[0]).then_inc(x_loaded, 16)
            load_head(0, 0)
            load_head(0, 1)
            load_prep(0)
            sp.dma_start(ctx_sb[:, :, :], ctx_dram[0]).then_inc(ctx_loaded, 16)
            load_prep(1)
            sp.dma_start(pad_sb[0:CH, P:3 * P], ssm).then_inc(ssm_loaded, 16)
            sp.dma_start(skip_sb[0:CH, :], skip.rearrange("(h a) -> h a", a=1)).then_inc(ssm_loaded, 16)
            sp.dma_start(lin_sb, lin_dram).then_inc(lin_loaded, 16)
            sp.dma_start(bias_sb[:, :], bias.rearrange("(a n) -> a n", a=1).partition_broadcast(P)).then_inc(y_free, 16)
            group(0, True, False)
            with sp.Fori(1, GROUPS - 1) as g:
                group(g, False, False)
            group(GROUPS - 1, False, True)
            store_y(GROUPS - 1)
            sp.wait_ge(y_free, 32 * GROUPS + 16)

        @block.gpsimd
        def _(pool):
            def split_head(g, h):
                r = h % 2
                after(pool, qk_done[1], g * HEADS + h - 1)
                pool.wait_ge(w_loaded[r], g * 16 * HEADS + 32 * (h // 2 + 1))
                raw = w_raw[:, r].rearrange("p m c n -> p (m c n)")
                hi = w_hi[:, r].rearrange("p m c n -> p (m c n)")
                lo = w_lo[:, r].rearrange("p m c n -> p (m c n)")
                nc.gpsimd.tensor_tensor(hi, raw, zeros[:, :], ALU.add).then_inc(w_hi_ready, 1)
                pool.wait_ge(w_hi_ready, g * HEADS + h + 1)
                nc.gpsimd.tensor_tensor(lo, raw, hi.bitcast(F32), ALU.subtract).then_inc(w_ready, 1)

            def power(k, n):
                pool.wait_ge(ln_var[k], n + 1)
                nc.gpsimd.tensor_tensor(rstd[:, k], veps[:, k], minus_half[:, :], ALU.pow).then_inc(ln_rstd[k], 1)

            def products(g, q):
                if q == 0:
                    pool.wait_ge(ctxT_saved, 2 * g + 2)
                after(pool, conv_done, g * CH + QH * (q - 1))
                for i in range(CI):
                    k_i = ctx_T[:, :, q * QH:(q + 1) * QH, :, i:i + 1].rearrange("p c h b i -> p c (h b) i")
                    k_j = ctx_T[:, :, q * QH:(q + 1) * QH, :, i:CI].rearrange("p c h b i -> p c (h b) i")
                    o = kv[:, q % 2, :, :, :, OFF[i]:OFF[i] + CI - i].rearrange("p c h b t -> p c (h b) t")
                    last = nc.gpsimd.tensor_tensor(o, k_i.to_broadcast([P, KC, QH * NB, CI - i]), k_j, ALU.mult)
                last.then_inc(kv_ready, 1)

            def gate(p, q, part):
                if part == 0:
                    pool.wait_ge(conv_saved, p * CH + QH * (q + 1))
                    if q == 1:
                        pool.wait_ge(ln2T_saved, 2 * p + 2)
                    else:
                        pool.wait_ge(mix_ready, 8 * p + 4)
                last = gate_part(nc.gpsimd, q, part)
                if part == 2:
                    last.then_inc(gated_ready[1], 1)

            def add_bias(p):
                pool.wait_ge(y_free, 32 * p + 16)
                pool.wait_ge(x3_ready, 2 * p + 2)
                nc.gpsimd.tensor_tensor(y[:, :, :], x2[:, :, :],
                                        bias_sb[:, :].rearrange("p (b n) -> p b n", b=1).to_broadcast([P, NB, DM]),
                                        ALU.add).then_inc(y_biased, 1)

            nc.gpsimd.memset(zeros[:, :], 0.0)
            nc.gpsimd.memset(minus_half[:, :], -0.5).then_inc(consts_ready, 1)
            nc.gpsimd.memset(pad_sb[0:CH, 0:P], 0.0).then_inc(pad_zeroed, 1)
            nc.gpsimd.memset(ident[:, :], 0.0).then_inc(consts_ready, 1)
            pool.wait_ge(consts_ready, 2)
            nc.gpsimd.affine_select(out=ident[:, :], in_=ident[:, :], compare_op=ALU.not_equal, fill=1.0,
                                    base=0, pattern=[[-1, P]], channel_multiplier=1).then_inc(consts_ready, 1)

            def group(g, first, last):
                for t in range(2, HEADS):
                    split_head(g, t)
                    if not first and 3 <= t <= 5:
                        gate(g - 1, 1, t - 3)
                    if not first and 8 <= t <= 10:
                        gate(g - 1, 3, t - 8)
                    if t == 11:
                        products(g, 0)
                    if t == 12:
                        products(g, 1)
                    if not first and t == 14:
                        power(2, g - 1)
                        add_bias(g - 1)
                    if not last and t == 15:
                        power(0, g + 1)
                if not last:
                    split_head(g + 1, 0)
                products(g, 2)
                if not last:
                    split_head(g + 1, 1)
                products(g, 3)
                power(1, g)

            split_head(0, 0)
            power(0, 0)
            split_head(0, 1)
            group(0, True, False)
            with pool.Fori(1, GROUPS - 1) as g:
                group(g, False, False)
            group(LAST, False, True)
            for q in (1, 3):
                for part in range(3):
                    gate(LAST, q, part)
            power(2, LAST)
            add_bias(LAST)

        @block.scalar
        def _(act):
            def xT_high(g):
                for c in range(KC):
                    act.wait_ge(xT_done, 2 * g + c + 1)
                    after(act, u_done, g * 4 * PAIRS)
                    nc.scalar.activation(xT_hi[:, c], (bank_q, bank_k)[c][:, :], ACT.Copy).then_inc(xT_hi_ready, 1)

            def save_qk(g, h, m):
                act.wait_ge(qk_done[m], g * HEADS + h + 1)
                after(act, scores_done, g * HEADS + h - 1)
                nc.scalar.activation(qk[:, m, h % 2], (bank_q, bank_k)[m][:, :], ACT.Copy,
                                     scale=(SCALE, 1.0)[m]).then_inc(qk_ready[m], 1)

            def exps(g, h):
                act.wait_ge(max_ready, g * HEADS + h + 1)
                after(act, col_done, g * HEADS + h - 1)
                for b in range(NB):
                    last = nc.scalar.activation(probs[:, h % 2, b], bank_s[:, b * SEQ:(b + 1) * SEQ], ACT.Exp,
                                                bias=neg_max[:, h, b:b + 1], accum_out=row_sum[:, h, b:b + 1])
                last.then_inc(probs_ready, 1)

            def save_ctxT(g):
                for c in range(KC):
                    act.wait_ge(ctxT_done, 2 * g + c + 1)
                    after(act, kv_ready, 4 * g)
                    nc.scalar.activation(ctx_T[:, c].rearrange("p h b i -> p b h i"),
                                         bank_x[c][:, :].rearrange("p (b h i) -> p b h i", b=NB, h=CH),
                                         ACT.Copy).then_inc(ctxT_saved, 1)

            def save_conv(p, h):
                act.wait_ge(conv_done, p * CH + h + 1)
                nc.scalar.activation(conv[:, :, h].rearrange("p c b t -> p c (b t)"),
                                     bank_x[h % 2][:, 0:KC * NB * TRI].rearrange("p (c n) -> p c n", c=KC),
                                     ACT.Copy).then_inc(conv_saved, 1)

            def save_ln2T(p):
                for c in range(KC):
                    act.wait_ge(ln2T_done, 2 * p + c + 1)
                    nc.scalar.activation(ln2_T[:, c].rearrange("p h b i -> p b h i"),
                                         bank_x[c][:, :].rearrange("p (b h i) -> p b h i", b=NB, h=CH),
                                         ACT.Copy).then_inc(ln2T_saved, 1)

            def save_ln3T(p):
                for c in range(KC):
                    act.wait_ge(ln3T_done, 2 * p + c + 1)
                    nc.scalar.activation(ln3_T[:, c], bank_x[c][:, :], ACT.Copy).then_inc(ln3T_saved, 1)

            def save_wvT(p):
                act.wait_ge(wvT_done, p + 1)
                nc.scalar.activation(wv_T[:, p % 2].rearrange("p h n -> p (h n)"), bank_x[0][:, :],
                                     ACT.Copy).then_inc(wvT_saved, 1)

            def m_high(p):
                for c in range(KC):
                    act.wait_ge(m_done, 2 * p + c + 1)
                    nc.scalar.activation(m_hi[:, c, p], bank_x[1 - c][:, :], ACT.Copy).then_inc(m_hi_ready, 1)

            def save_linT():
                act.wait_ge(linT_done, 1)
                nc.scalar.activation(lin_T[:, :, :].rearrange("p c n -> p (c n)"), bank_x[0][:, :],
                                     ACT.Copy).then_inc(linT_saved, 1)

            def group(g, first, last):
                for t in range(STEPS):
                    if t < HEADS:
                        save_qk(g, t, 0)
                        save_qk(g, t, 1)
                    if 1 <= t <= HEADS:
                        exps(g, t - 1)
                    if t == 4:
                        save_ctxT(g)
                    if first:
                        if t < HEADS and t % 2 == 0:
                            save_wvT(t // 2)
                        if t < HEADS and t % 2 == 1:
                            m_high(t // 2)
                        if t == 15:
                            save_linT()
                    else:
                        if t == 1:
                            save_ln2T(g - 1)
                        if t == 15:
                            save_ln3T(g - 1)
                    for h in CONV_AT.get(t, ()):
                        save_conv(g, h)
                if not last:
                    xT_high(g + 1)
                for h in CONV_AT[STEPS]:
                    save_conv(g, h)

            xT_high(0)
            group(0, True, False)
            with act.Fori(1, GROUPS - 1) as g:
                group(g, False, False)
            group(GROUPS - 1, False, True)
            save_ln2T(GROUPS - 1)
            save_ln3T(GROUPS - 1)

        @block.vector
        def _(dve):
            def ln_moments(k, n, src):
                for b in range(NB):
                    last = nc.vector.bn_stats(stats[:, k, b], src[:, b])
                last.then_inc(ln_stats[k], 1)
                dve.wait_ge(ln_stats[k], n + 1)
                nc.vector.tensor_copy(pace[:, 0:1], stats[:, k, 0, 0:1])
                for b in range(NB):
                    last = nc.vector.bn_aggr(mv[:, k, b], stats[:, k, b])
                last.then_inc(ln_mv[k], 1)
                dve.wait_ge(ln_mv[k], n + 1)
                nc.vector.tensor_scalar(veps[:, k], mv[:, k, :, 1], EPS, None, ALU.add).then_inc(ln_var[k], 1)

            def ln_normalise(k, n, src, dst):
                dve.wait_ge(ln_rstd[k], n + 1)
                for b in range(NB):
                    last = nc.vector.tensor_scalar(dst[:, b], src[:, b], mv[:, k, b, 0:1], rstd[:, k, b:b + 1],
                                                   ALU.subtract, ALU.mult)
                last.then_inc(ln_ready[k], 1)

            def xT_low(g):
                for c in range(KC):
                    dve.wait_ge(xT_hi_ready, 2 * g + c + 1)
                    nc.vector.tensor_tensor(xT_lo[:, c], (bank_q, bank_k)[c][:, :], xT_hi[:, c].bitcast(F32),
                                            ALU.subtract).then_inc(xT_ready, 1)

            def row_max(g, h):
                dve.wait_ge(scores_done, g * HEADS + h + 1)
                nc.vector.tensor_reduce(out=neg_max[:, h], in_=bank_s[:, :].rearrange("p (b k) -> p b k", b=NB),
                                        op=ALU.max, axis=AX.X, negate=True).then_inc(max_ready, 1)

            def row_inverse(g, h):
                dve.wait_ge(probs_ready, g * HEADS + h + 1)
                nc.vector.reciprocal(row_inv[:, h], row_sum[:, h]).then_inc(inv_ready, 1)

            def save_col(g, h):
                dve.wait_ge(col_done, g * HEADS + h + 1)
                nc.vector.tensor_copy(col_sum[:, h], bank_c[:, 0:NB]).then_inc(col_ready, 1)

            def add_u(g, p, b):
                n = g * 4 * PAIRS + NB * p + b
                dve.wait_ge(u_done, n + 1)
                dve.wait_ge(col_ready, g * HEADS + 2 * p + 2)
                for j in range(2):
                    h = 2 * p + j
                    if j == 1:
                        dve.wait_ge(u_added, 2 * n + 1)
                    nc.vector.scalar_tensor_tensor(
                        out=(x2 if h == HEADS - 1 else acc)[:, b], in0=bank_u[b % 2][:, j * DM:(j + 1) * DM],
                        scalar=col_sum[:, h, b:b + 1], in1=(x_in if h == 0 else acc)[:, b],
                        op0=ALU.mult, op1=ALU.add).then_inc(u_added, 1)

            def gate(p, q, part):
                if part == 0:
                    if q == 0:
                        dve.wait_ge(ln2T_saved, 2 * p + 2)
                    else:
                        dve.wait_ge(mix_ready, 8 * p + 2)
                    dve.wait_ge(conv_saved, p * CH + QH * (q + 1))
                last = gate_part(nc.vector, q, part)
                if part == 2:
                    last.then_inc(gated_ready[0], 1)

            def mix(p, q, c):
                dve.wait_ge(gated_ready[q % 2], 2 * p + q // 2 + 1)
                nc.vector.tensor_reduce(
                    out=mixT[:, c, :, q * QH:(q + 1) * QH].rearrange("p b h j -> p h b j"),
                    in_=gated[q % 2][:, c].rearrange("p (h b) j i -> p h b j i", h=QH), op=ALU.add,
                    axis=AX.X).then_inc(mix_ready, 1)

            def mixing_piece(p, piece):
                what, q, part = piece
                (gate if what == "gate" else mix)(p, q, part)

            def add_mix(p):
                for s in range(2):
                    dve.wait_ge(back_done, 2 * p + s + 1)
                    t = x2[:, 2 * s:2 * s + 2].rearrange("p b n -> p (b n)")
                    nc.vector.tensor_tensor(t, bank_x[s][:, :], t, ALU.add).then_inc(x3_ready, 1)

            def add_lin(p):
                dve.wait_ge(y_biased, p + 1)
                for s in range(2):
                    dve.wait_ge(lin_done, 2 * p + s + 1)
                    t = y[:, 2 * s:2 * s + 2].rearrange("p b n -> p (b n)")
                    nc.vector.tensor_tensor(t, bank_x[s][:, :], t, ALU.add).then_inc(y_ready, 1)

            def m_low(p):
                for c in range(KC):
                    dve.wait_ge(m_hi_ready, 2 * p + c + 1)
                    nc.vector.tensor_tensor(m_lo[:, c, p], bank_x[1 - c][:, :], m_hi[:, c, p].bitcast(F32),
                                            ALU.subtract).then_inc(m_ready, 1)

            def binarise():
                dve.wait_ge(lin_loaded, 16)
                nc.vector.tensor_reduce(out=alpha[:, :], in_=lin_sb, op=ALU.add, axis=AX.X,
                                        apply_absolute_value=True).then_inc(lin_step, 1)
                nc.vector.tensor_scalar(lin_bin, lin_sb, 0.0, 2.0, ALU.is_ge, ALU.mult).then_inc(lin_step, 1)
                dve.wait_ge(lin_step, 2)
                nc.vector.tensor_scalar(alpha[:, :], alpha[:, :], 1.0 / DM, None, ALU.mult).then_inc(lin_step, 1)
                dve.wait_ge(lin_step, 3)
                for o in range(KC):
                    nc.vector.tensor_scalar(lin_bin[:, o], lin_bin[:, o], -1.0, alpha[:, o:o + 1],
                                            ALU.add, ALU.mult).then_inc(lin_step, 1)
                dve.wait_ge(lin_step, 5)
                nc.vector.tensor_tensor(lin_bin, lin_bin, lin_sb, ALU.subtract).then_inc(lin_step, 1)
                dve.wait_ge(lin_step, 6)
                nc.vector.tensor_tensor(lin_bin, lin_bin, lin_sb, ALU.add).then_inc(lin_ready, 1)

            def group(g, first, last):
                for t in range(STEPS):
                    if 1 <= t <= HEADS:
                        row_max(g, t - 1)
                    if t >= 4:
                        add_u(g, (t - 4) // 2, 2 * (t % 2))
                    if not first and t in MIXING_AT:
                        mixing_piece(g - 1, MIXING_AT[t][0])
                    if 1 <= t <= HEADS:
                        row_inverse(g, t - 1)
                    if 2 <= t <= HEADS + 1:
                        save_col(g, t - 2)
                    if t >= 4:
                        add_u(g, (t - 4) // 2, 2 * (t % 2) + 1)
                    if not first and len(MIXING_AT.get(t, ())) > 1:
                        mixing_piece(g - 1, MIXING_AT[t][1])
                    if first:
                        if t < HEADS and t % 2 == 1:
                            m_low(t // 2)
                        if t == 10:
                            binarise()
                    else:
                        if t == 0:
                            ln_normalise(1, g - 1, x2, ln23)
                        if t == 12:
                            add_mix(g - 1)
                            dve.wait_ge(x3_ready, 2 * g)
                            ln_moments(2, g - 1, x2)
                        if t == 13:
                            ln_normalise(2, g - 1, x2, ln23)
                        if t == 15:
                            add_lin(g - 1)
                    if not last:
                        if t == 13:
                            dve.wait_ge(x_loaded, 16 * g + 32)
                            ln_moments(0, g + 1, x_in)
                        if t == 15:
                            ln_normalise(0, g + 1, x_in, ln1)
                if not last:
                    xT_low(g + 1)
                dve.wait_ge(u_added, g * 8 * PAIRS + 8 * PAIRS)
                ln_moments(1, g, x2)

            dve.wait_ge(x_loaded, 16)
            ln_moments(0, 0, x_in)
            ln_normalise(0, 0, x_in, ln1)
            xT_low(0)
            dve.wait_ge(ssm_loaded, 32)
            dve.wait_ge(pad_zeroed, 1)
            nc.vector.tensor_tensor(pad_sb[0:CH, P:P + 1], pad_sb[0:CH, P:P + 1], skip_sb[0:CH, :],
                                    ALU.add).then_inc(pad_ready, 1)
            group(0, True, False)
            with dve.Fori(1, GROUPS - 1) as g:
                group(g, False, False)
            group(GROUPS - 1, False, True)
            p = GROUPS - 1
            ln_normalise(1, p, x2, ln23)
            for t in sorted(MIXING_AT):
                for piece in MIXING_AT[t]:
                    mixing_piece(p, piece)
            add_mix(p)
            dve.wait_ge(x3_ready, 2 * GROUPS)
            ln_moments(2, p, x2)
            ln_normalise(2, p, x2, ln23)
            add_lin(p)

        @block.tensor
        def _(pe):
            def three(out_, a_hi, a_lo, b_hi, b_lo, start, stop):
                nc.tensor.matmul(out_, a_hi, b_hi, start=start, stop=False)
                nc.tensor.matmul(out_, a_hi, b_lo, start=False, stop=False)
                return nc.tensor.matmul(out_, a_lo, b_hi, start=False, stop=stop)

            def transpose_tiles(src, done, banks=bank_x):
                for c in range(KC):
                    for b in range(NB):
                        last = nc.tensor.transpose(banks[c][:, b * P:(b + 1) * P], src[:, b, c * P:(c + 1) * P],
                                                   ident[:, :])
                    last.then_inc(done, 1)

            def project(g, h, m):
                if m == 0:
                    pe.wait_ge(w_ready, g * HEADS + h + 1)
                after(pe, qk_ready[m], g * HEADS + h)
                for c in range(KC):
                    last = three((bank_q, bank_k)[m][:, :], w_hi[:, h % 2, m, c], w_lo[:, h % 2, m, c],
                                 xT_hi[:, c], xT_lo[:, c], c == 0, c == KC - 1)
                last.then_inc(qk_done[m], 1)

            def scores(g, h):
                pe.wait_ge(qk_ready[0], g * HEADS + h + 1)
                pe.wait_ge(qk_ready[1], g * HEADS + h + 1)
                after(pe, probs_ready, g * HEADS + h)
                r = h % 2
                for b in range(NB):
                    s = slice(b * SEQ, (b + 1) * SEQ)
                    last = nc.tensor.matmul(bank_s[:, s], qk[:, 0, r, s], qk[:, 1, r, s], start=True, stop=True)
                last.then_inc(scores_done, 1)

            def column_sums(g, h):
                pe.wait_ge(inv_ready, g * HEADS + h + 1)
                after(pe, col_ready, g * HEADS + h)
                for b in range(NB):
                    last = nc.tensor.matmul(bank_c[:, b:b + 1], probs[:, h % 2, b], row_inv[:, h, b:b + 1],
                                            start=True, stop=True)
                last.then_inc(col_done, 1)

            def values(g, p, b):
                n = g * 4 * PAIRS + NB * p + b
                after(pe, u_added, 2 * n - 2)
                s = slice(b * P, (b + 1) * P)
                for c in range(KC):
                    last = three(bank_u[b % 2][:, :], xT_hi[:, c, s], xT_lo[:, c, s], m_hi[:, c, p], m_lo[:, c, p],
                                 c == 0, c == KC - 1)
                last.then_inc(u_done, 1)

            def convolve(p, h):
                if h % QH == 0:
                    pe.wait_ge(kv_ready, 4 * p + h // QH + 1)
                if h >= 2:
                    pe.wait_ge(conv_saved, p * CH + h - 1)
                src = kv[:, (h // QH) % 2, :, h % QH].rearrange("p c b t -> p c (b t)")
                n = NB * TRI
                near, far = toeplitz[:, h, 0:P], toeplitz[:, h, P:2 * P]
                o = bank_x[h % 2]
                nc.tensor.matmul(o[:, 0:n], near, src[:, 0], start=True, stop=True)
                nc.tensor.matmul(o[:, n:2 * n], near, src[:, 1], start=True, stop=False)
                nc.tensor.matmul(o[:, n:2 * n], far, src[:, 0], start=False, stop=True).then_inc(conv_done, 1)

            def transpose_ln2(p):
                pe.wait_ge(ln_ready[1], p + 1)
                pe.wait_ge(conv_saved, p * CH + CH)
                transpose_tiles(ln23, ln2T_done)

            def transpose_back(p):
                pe.wait_ge(mix_ready, 8 * (p + 1))
                pe.wait_ge(ln2T_saved, 2 * p + 2)
                for s in range(2):
                    for b in range(2 * s, 2 * s + 2):
                        for c in range(KC):
                            last = nc.tensor.transpose(bank_x[s][:, (b % 2) * DM + c * P:(b % 2) * DM + (c + 1) * P],
                                                       mixT[:, c, b].rearrange("p h j -> p (h j)"), ident[:, :])
                    last.then_inc(back_done, 1)

            def transpose_ln3(p):
                pe.wait_ge(ln_ready[2], p + 1)
                transpose_tiles(ln23, ln3T_done)

            def linear(p):
                pe.wait_ge(ln3T_saved, 2 * p + 2)
                for s in range(2):
                    for b in range(2 * s, 2 * s + 2):
                        for c in range(KC):
                            last = nc.tensor.matmul(bank_x[s][:, (b % 2) * DM:(b % 2 + 1) * DM],
                                                    ln3_T[:, c, b * P:(b + 1) * P], lin_T[:, c],
                                                    start=c == 0, stop=c == KC - 1)
                    last.then_inc(lin_done, 1)

            def transpose_wv(p):
                pe.wait_ge(prep_loaded[p % 2], 32 * (p // 2 + 1))
                if p == 2:
                    pe.wait_ge(ctxT_saved, 2)
                elif p > 0:
                    pe.wait_ge(m_ready, 2 * p)
                for j in range(2):
                    for c in range(KC):
                        last = nc.tensor.transpose(bank_x[0][:, (2 * j + c) * P:(2 * j + c + 1) * P],
                                                   wv_sb[:, p % 2, c, j * HD:(j + 1) * HD], ident[:, :])
                last.then_inc(wvT_done, 1)

            def multiply_wv_wo(p):
                pe.wait_ge(wvT_saved, p + 1)
                for c in range(KC):
                    for j in range(2):
                        last = nc.tensor.matmul(bank_x[1 - c][:, j * DM:(j + 1) * DM], wv_T[:, p % 2, j, c * P:(c + 1) * P],
                                                wo_sb[:, p % 2, j], start=True, stop=True)
                    last.then_inc(m_done, 1)

            def transpose_lin():
                pe.wait_ge(lin_ready, 1)
                pe.wait_ge(m_ready, 2 * PAIRS)
                for c in range(KC):
                    for o in range(KC):
                        last = nc.tensor.transpose(bank_x[0][:, (2 * c + o) * P:(2 * c + o + 1) * P],
                                                   lin_bin[:, o, c * P:(c + 1) * P], ident[:, :])
                last.then_inc(linT_done, 1)

            def first_conv(g, first):
                if first:
                    pe.wait_ge(linT_saved, 1)
                    pe.wait_ge(toeplitz_loaded, 16)
                else:
                    pe.wait_ge(y_ready, 2 * g)

            def transpose_next_x(g):
                pe.wait_ge(ln_ready[0], g + 1)
                after(pe, qk_ready[0], g * HEADS)
                after(pe, qk_ready[1], g * HEADS)
                transpose_tiles(ln1, xT_done, (bank_q, bank_k))

            def group(g, first, last):
                pe.wait_ge(xT_ready, 2 * g + 2)
                for t in range(STEPS):
                    if t < HEADS:
                        project(g, t, 0)
                        project(g, t, 1)
                    if 1 <= t <= HEADS:
                        scores(g, t - 1)
                    if t >= 4:
                        if first and t % 2 == 0:
                            pe.wait_ge(m_ready, 2 * ((t - 4) // 2) + 2)
                        values(g, (t - 4) // 2, 2 * (t % 2))
                    if 2 <= t <= HEADS + 1:
                        column_sums(g, t - 2)
                    if t >= 4:
                        values(g, (t - 4) // 2, 2 * (t % 2) + 1)
                    if t == 4:
                        if first:
                            pe.wait_ge(m_ready, 4)
                        else:
                            pe.wait_ge(ln2T_saved, 2 * g)
                        pe.wait_ge(ctx_loaded, 16 * g + 16)
                        transpose_tiles(ctx_sb, ctxT_done)
                    if first:
                        if t < HEADS and t % 2 == 0:
                            transpose_wv(t // 2)
                        if t < HEADS and t % 2 == 1:
                            multiply_wv_wo(t // 2)
                        if t == 15:
                            transpose_lin()
                    else:
                        if t == 1:
                            transpose_ln2(g - 1)
                        if t == 11:
                            pe.wait_ge(ctxT_saved, 2 * g + 2)
                            transpose_back(g - 1)
                        if t == 14:
                            transpose_ln3(g - 1)
                        if t == 15:
                            linear(g - 1)
                    if t == min(CONV_AT):
                        first_conv(g, first)
                    for h in CONV_AT.get(t, ()):
                        convolve(g, h)
                    if t == 17 and not last:
                        transpose_next_x(g + 1)
                for h in CONV_AT[STEPS]:
                    convolve(g, h)

            pe.wait_ge(consts_ready, 3)
            transpose_next_x(0)
            group(0, True, False)
            with pe.Fori(1, GROUPS - 1) as g:
                group(g, False, False)
            group(GROUPS - 1, False, True)
            transpose_ln2(LAST)
            transpose_back(LAST)
            transpose_ln3(LAST)
            linear(LAST)


_INS = ["x", "ctx_2048", "L0_attn_w_qkv", "L0_attn_w_o", "L0_xattn_ssm_kernel", "L0_xattn_D", "L0_ffn_weight",
        "L0_ffn_bias"]


def kernel(**inputs):
    import numpy as _np
    import concourse.bacc as _bacc
    from concourse import mybir as _mybir
    from concourse.bass_utils import run_bass_kernel_spmd as _run

    nc = _bacc.Bacc("TRN2", target_bir_lowering=False, num_devices=1)
    arrays, args = {}, []
    for name in _INS:
        a = _np.ascontiguousarray(inputs[name])
        arrays[f"in_{name}"] = a
        args.append(nc.dram_tensor(f"in_{name}", a.shape, _mybir.dt.from_np(a.dtype), kind="ExternalInput").ap())
    args.append(nc.dram_tensor("out_0", inputs["x"].shape, _mybir.dt.float32, kind="ExternalOutput").ap())
    decoder_layer(nc, *args)
    r = _run(nc, [arrays], core_ids=[0])
    return r.results[0]["out_0"]
```

```python
import concourse.bass as bass
from concourse import mybir
from contextlib import ExitStack

F32 = mybir.dt.float32
FR = mybir.dt.float32r
ALU = mybir.AluOpType
ACT = mybir.ActivationFunctionType
AX = mybir.AxisListType


def decoder_layer(nc, x, ctx_in, w_qkv, w_o, ssm, skip, w_lin, bias, out):
    P = 128
    NSEQ, SEQ, DM = x.shape
    HD = P
    HEADS = w_o.shape[0] // HD
    PAIRS = HEADS // 2
    KC = DM // P
    NB = 4
    GROUPS = NSEQ // NB
    LAST = GROUPS - 1
    TOK = NB * SEQ
    SCALE = float(HD) ** -0.5
    EPS = 1e-5
    CH = ssm.shape[0]
    CI = P // CH
    TRI = CI * (CI + 1) // 2
    OFF = [i * CI - i * (i - 1) // 2 for i in range(CI)]
    QH = CH // 4
    VBUF = 4

    OWN = {(7, 0): ("ctx", 0), (7, 1): ("ctx", 1)}
    for h, at in enumerate([(10, 2), (11, 1), (11, 2), (11, 3), (12, 0), (12, 1), (12, 2), (12, 3), (13, 2), (13, 3),
                            (14, 2), (14, 3), (15, 0), (15, 1), (15, 2), (15, 3)]):
        OWN[at] = ("conv", h)
    FORMER = {(5, 0): ("ln2", 0), (5, 2): ("ln2", 1), (10, 3): ("back", 0),
              (11, 0): ("back", 1), (13, 0): ("ln3", 0), (13, 1): ("ln3", 1), (14, 0): ("lin", 0), (14, 1): ("lin", 1)}
    LATE = dict(zip([(0, 1), (0, 2), (0, 3), (1, 1), (1, 2), (1, 3), (2, 1), (2, 3), (3, 0), (3, 1)],
                    [("conv", h) for h in range(6, CH)]))
    USES = {"first": {**OWN, (6, 2): ("lin_w", 0)}, "middle": {**OWN, **FORMER},
            "last": {at: use for at, use in {**OWN, **FORMER}.items() if use not in LATE.values()},
            "after": {**LATE, (5, 0): ("ln2", 0), (5, 1): ("ln2", 1), (10, 0): ("back", 0), (10, 1): ("back", 1),
                      (11, 0): ("ln3", 0), (11, 1): ("lin", 0), (12, 0): ("ln3", 1), (12, 1): ("lin", 1)}}
    MIX_EARLY = {5: [("gate", 0, 0), ("gate", 0, 1)], 6: [("mix", 0, 0)], 7: [("mix", 0, 1)], 8: [("gate", 2, 2)],
                 9: [("mix", 2, 1)], 10: [("mix", 3, 1)]}
    MIX_LATE = {5: [("gate", 0, 2)], 6: [("mix", 1, 0), ("mix", 1, 1)], 7: [("gate", 2, 0), ("gate", 2, 1)],
                8: [("mix", 2, 0)], 9: [("mix", 3, 0)]}
    GATE_POOL = {6: [(1, 0), (1, 1)], 7: [(1, 2)], 8: [(3, 0)], 9: [(3, 1), (3, 2)]}

    def bank_turn(kind, g, use):
        first, middle = len(USES["first"]), len(USES["middle"])
        before = 0 if kind == "first" else (g - 1) * middle + first
        if kind == "after":
            before -= middle - len(USES["last"])
        order = [USES[kind][at] for at in sorted(USES[kind])]
        return before + order.index(use) + 1

    def runs(kind, h):
        return {"first": h >= 0, "middle": True, "last": True, "after": h < 0}[kind]

    ctx = ExitStack()
    with ctx:
        def sb(name, shape, dt=F32):
            return ctx.enter_context(nc.sbuf_tensor(name, [P] + shape, dt))

        def bank(name):
            return ctx.enter_context(nc.psum_tensor(name, [P, 512], F32))

        def sem(name):
            return ctx.enter_context(nc.semaphore(name))

        ident = sb("ident", [P])
        zero = sb("zero", [1])
        one = sb("one", [1])
        zero_r = sb("zero_r", [1], FR)
        one_r = sb("one_r", [1], FR)
        minus_half = sb("minus_half", [NB])
        toeplitz = sb("toeplitz", [CH, 2 * P])
        wv_hi = sb("wv_hi", [KC, HEADS * HD], FR)
        wv_lo = sb("wv_lo", [KC, HEADS * HD], FR)
        wo_hi = sb("wo_hi", [HEADS, DM], FR)
        wo_lo = sb("wo_lo", [HEADS, DM], FR)
        lin_hi = sb("lin_hi", [KC, DM], FR)
        lin_lo = sb("lin_lo", [KC, DM], FR)
        bias_sb = sb("bias_sb", [DM])
        w_raw = sb("w_raw", [2, 2, KC, HD])
        w_hi = sb("w_hi", [2, 2, KC, HD], FR)
        w_lo = sb("w_lo", [2, 2, KC, HD], FR)
        inputs = sb("inputs", [2, NB, DM])
        x_in, ctx_sb = inputs[:, 0], inputs[:, 1]
        xT_hi = sb("xT_hi", [KC, TOK], FR)
        xT_lo = sb("xT_lo", [KC, TOK], FR)
        qk = sb("qk", [2, 2, TOK])
        probs = sb("probs", [NB, SEQ])
        neg_max = sb("neg_max", [2, NB])
        row_sum = sb("row_sum", [2, NB])
        row_inv = sb("row_inv", [2, NB])
        probs_hi = sb("probs_hi", [2, NB, SEQ], FR)
        probs_lo = sb("probs_lo", [2, NB, SEQ], FR)
        v_sb = sb("v_sb", [VBUF, TOK])
        vals_hi = sb("vals_hi", [TOK], FR)
        vals_lo = sb("vals_lo", [TOK], FR)
        ctx_T = sb("ctx_T", [KC, CH, NB, CI])
        kv_mem = sb("kv_mem", [2 * KC * QH * NB * TRI])
        kv = kv_mem[:, :].rearrange("p (r c h b t) -> p r c h b t", r=2, c=KC, h=QH, b=NB)
        conv = sb("conv", [KC, CH, NB, TRI])
        def as_gated(flat):
            return flat.rearrange("p (n j i) -> p n j i", j=CI, i=CI)
        gated0 = as_gated(kv_mem[:, 0:KC * CH * CI * CI])
        gated1 = sb("gated1", [KC * CH, CI, CI])
        gated2 = as_gated(inputs[:, :, :, :].rearrange("p r b n -> p (r b n)"))
        GATED = {"middle": [gated0, gated1, gated0, gated1], "last": [gated0, gated1, gated0, gated1],
                 "after": [gated0, gated1, gated0, gated2]}
        x2 = sb("x2", [NB, DM])
        ln = sb("ln", [NB, DM])
        ln2_T = sb("ln2_T", [KC, CH, NB, CI])
        ln3_hi = sb("ln3_hi", [KC, TOK], FR)
        ln3_lo = sb("ln3_lo", [KC, TOK], FR)
        y = sb("y", [NB, DM])
        stats = sb("stats", [3, NB, 6])
        mv = sb("mv", [3, NB, 2])
        veps = sb("veps", [3, NB])
        rstd = sb("rstd", [3, NB])
        pace = sb("pace", [4])
        flat0 = gated1[:, :, :, :].rearrange("p n j i -> p (n j i)")
        flat1 = kv_mem
        WB = KC * 2 * HD
        wv_sb = flat0[:, 0:2 * WB].rearrange("p (r c n) -> p r c n", r=2, c=KC)
        wo_sb = flat0[:, 2 * WB:4 * WB].rearrange("p (r h n) -> p r h n", r=2, h=2)
        lin_sb = flat1[:, 0:WB].rearrange("p (o n) -> p o n", o=KC)
        lin_bin = flat1[:, WB:2 * WB].rearrange("p (o n) -> p o n", o=KC)
        alpha = sb("alpha", [KC])
        pad_sb = flat1[:, 2 * WB:2 * WB + 3 * P]
        skip_sb = sb("skip_sb", [1])
        pad_dram = nc.dram_tensor("padded_kernel", [CH, 3 * P], F32, kind="Internal")
        rows_dram = nc.dram_tensor("toeplitz_rows", [P, CH, 2 * P], F32, kind="Internal")

        bank_qk = [bank("bank_q"), bank("bank_k")]
        bank_s, bank_v, bank_c = bank("bank_s"), bank("bank_v"), bank("bank_c")
        bank_o = [bank("bank_o0"), bank("bank_o1")]
        bank_x = bank("bank_x")

        x_loaded = [sem("x_loaded0"), sem("x_loaded1")]
        x2_loaded, ctx_loaded = sem("x2_loaded"), sem("ctx_loaded")
        w_loaded = [sem("w_loaded0"), sem("w_loaded1")]
        prep_loaded = [sem("prep_loaded0"), sem("prep_loaded1")]
        lin_loaded, ssm_loaded = sem("lin_loaded"), sem("ssm_loaded")
        pad_stored, rows_stored, toeplitz_loaded = sem("pad_stored"), sem("rows_stored"), sem("toeplitz_loaded")
        y_free = sem("y_free")
        ln_stats = [sem(f"ln_stats{k}") for k in range(3)]
        ln_mv = [sem(f"ln_mv{k}") for k in range(3)]
        ln_var = [sem(f"ln_var{k}") for k in range(3)]
        ln_rstd = [sem(f"ln_rstd{k}") for k in range(3)]
        ln_ready = [sem(f"ln_ready{k}") for k in range(3)]
        xT_done, xT_hi_ready, xT_ready = sem("xT_done"), sem("xT_hi_ready"), sem("xT_ready")
        w_hi_ready, w_ready = sem("w_hi_ready"), sem("w_ready")
        qk_done = [sem("q_done"), sem("k_done")]
        qk_ready = [sem("q_ready"), sem("k_ready")]
        scores_done, max_ready, probs_ready = sem("scores_done"), sem("max_ready"), sem("probs_ready")
        inv_ready, col_done = sem("inv_ready"), sem("col_done")
        divided, probs_hi_ready, probs_lo_ready = sem("divided"), sem("probs_hi_ready"), sem("probs_lo_ready")
        v_done, v_saved = sem("v_done"), sem("v_saved")
        vals_ready, vals_hi_ready, vals_lo_ready = sem("vals_ready"), sem("vals_hi_ready"), sem("vals_lo_ready")
        att_done, x2_summed = sem("att_done"), sem("x2_summed")
        x_written, x_read = sem("x_written"), sem("x_read")
        x_hi_ready = sem("x_hi_ready")
        kv_ready = sem("kv_ready")
        gated_ready, mix_ready = [sem("gated_ready0"), sem("gated_ready1")], sem("mix_ready")
        y_biased = sem("y_biased")
        consts_ready, pad_zeroed, pad_ready = sem("consts_ready"), sem("pad_zeroed"), sem("pad_ready")
        lin_step, lin_ready = sem("lin_step"), sem("lin_ready")
        prep_hi_ready, prep_ready = sem("prep_hi_ready"), sem("prep_ready")

        def after(eng, signal, count):
            if not isinstance(count, int) or count > 0:
                eng.wait_ge(signal, count)

        def gate_part(eng, kind, b, part):
            pc = conv[:, :, :, b].rearrange("p c h t -> p (c h) t")
            qc = ln2_T[:, :, :, b].rearrange("p c h i -> p (c h) i")
            o = GATED[kind][b]
            if part < 2:
                for i in (range(3), range(3, CI))[part]:
                    last = eng.tensor_tensor(o[:, :, i:CI, i], pc[:, :, OFF[i]:OFF[i] + CI - i],
                                             qc[:, :, i:i + 1].to_broadcast([P, KC * CH, CI - i]), ALU.mult)
            else:
                for j in range(CI - 1):
                    last = eng.tensor_tensor(o[:, :, j, j + 1:CI], pc[:, :, OFF[j] + 1:OFF[j] + CI - j],
                                             qc[:, :, j + 1:CI], ALU.mult)
            return last

        x_dram = x.rearrange("(g b) s d -> g s b d", b=NB)
        ctx_dram = ctx_in.rearrange("(g b) s d -> g s b d", b=NB)
        out_dram = out.rearrange("(g b) s d -> g s b d", b=NB)
        w_dram = w_qkv.rearrange("(c p) (m n) -> m p c n", p=P, m=3)
        wo_dram = w_o.rearrange("(h d) n -> d h n", d=HD)
        lin_dram = w_lin.rearrange("(o p) n -> p o n", p=P)

        block = ctx.enter_context(nc.Block())

        @block.sync
        def _(sp):
            def load_head(g, h):
                after(sp, w_ready, g * HEADS + h - 1)
                for m in range(2):
                    sp.dma_start(w_raw[:, h % 2, m], w_dram[m, :, :, h * HD:(h + 1) * HD]).then_inc(w_loaded[h % 2], 16)

            def load_x(g):
                for s in range(2):
                    sp.dma_start(x_in[:, 2 * s:2 * s + 2], x_dram[g, :, 2 * s:2 * s + 2]).then_inc(x_loaded[s], 16)

            def load_prep(p):
                after(sp, prep_ready, 2 * (p - 1))
                loaded = prep_loaded[p % 2]
                sp.dma_start(wv_sb[:, p % 2], w_dram[2, :, :, 2 * p * HD:(2 * p + 2) * HD]).then_inc(loaded, 16)
                sp.dma_start(wo_sb[:, p % 2], wo_dram[:, 2 * p:2 * p + 2, :]).then_inc(loaded, 16)

            def store_y(kind, g):
                p = g - 1
                for s in range(2):
                    sp.wait_ge(x_read, bank_turn(kind, g, ("lin", s)))
                    sp.dma_start(out_dram[p, :, 2 * s:2 * s + 2], y[:, 2 * s:2 * s + 2]).then_inc(y_free, 16)

            def toeplitz_part(n):
                if n == 0:
                    sp.wait_ge(pad_ready, 1)
                    sp.dma_start(pad_dram[:, :], pad_sb[0:CH, :]).then_inc(pad_stored, 16)
                elif n == 1:
                    sp.wait_ge(pad_stored, 16)
                    sp.dma_start(rows_dram[:, :, :].rearrange("l h m -> h l m"),
                                 bass.AP(pad_dram, P, [[3 * P, CH], [-1, P], [1, 2 * P]])).then_inc(rows_stored, 16)
                else:
                    sp.wait_ge(rows_stored, 16)
                    sp.dma_start(toeplitz[:, :, :], rows_dram[:, :, :]).then_inc(toeplitz_loaded, 16)

            def group(kind, g, last):
                for h in range(2, HEADS):
                    load_head(g, h)
                    if kind == "first" and h % 2 == 1 and h // 2 + 1 < PAIRS:
                        load_prep(h // 2 + 1)
                    if kind == "first" and h in (4, 6, 8):
                        toeplitz_part(h // 2 - 2)
                    if h == 5 and not last:
                        sp.wait_ge(xT_ready, 2 * g + 2)
                        load_x(g + 1)
                    if h == 10 and not last:
                        sp.wait_ge(x_written, bank_turn(kind, g, ("ctx", 1)))
                        sp.dma_start(ctx_sb[:, :, :], ctx_dram[g + 1]).then_inc(ctx_loaded, 16)
                if not last:
                    load_head(g + 1, 0)
                    load_head(g + 1, 1)
                if kind != "first":
                    sp.wait_ge(y_biased, 2 * g)
                    sp.wait_ge(ln_ready[2], 2 * g)
                    sp.dma_start(x2[:, :, :], x_dram[g]).then_inc(x2_loaded, 16)
                    store_y(kind, g)

            load_x(0)
            load_head(0, 0)
            load_head(0, 1)
            load_prep(0)
            load_prep(1)
            sp.dma_start(ctx_sb[:, :, :], ctx_dram[0]).then_inc(ctx_loaded, 16)
            sp.dma_start(pad_sb[0:CH, P:3 * P], ssm).then_inc(ssm_loaded, 16)
            sp.dma_start(skip_sb[0:CH, :], skip.rearrange("(h a) -> h a", a=1)).then_inc(ssm_loaded, 16)
            sp.dma_start(lin_sb, lin_dram).then_inc(lin_loaded, 16)
            sp.dma_start(bias_sb[:, :], bias.rearrange("(a n) -> a n", a=1).partition_broadcast(P)).then_inc(y_free, 16)
            sp.dma_start(x2[:, :, :], x_dram[0]).then_inc(x2_loaded, 16)
            group("first", 0, False)
            with sp.Fori(1, LAST) as g:
                group("middle", g, False)
            group("last", LAST, True)
            store_y("after", GROUPS)
            sp.wait_ge(y_free, 32 * GROUPS + 16)

        @block.gpsimd
        def _(pool):
            def split_head(g, h):
                r = h % 2
                after(pool, qk_done[1], g * HEADS + h - 1)
                pool.wait_ge(w_loaded[r], g * 16 * HEADS + 32 * (h // 2 + 1))
                raw = w_raw[:, r].rearrange("p m c n -> p (m c n)")
                hi = w_hi[:, r].rearrange("p m c n -> p (m c n)")
                lo = w_lo[:, r].rearrange("p m c n -> p (m c n)")
                nc.gpsimd.tensor_tensor(hi, raw, zero[:, :].to_broadcast([P, 2 * KC * HD]),
                                        ALU.add).then_inc(w_hi_ready, 1)
                pool.wait_ge(w_hi_ready, g * HEADS + h + 1)
                nc.gpsimd.tensor_tensor(lo, raw, hi.bitcast(F32), ALU.subtract).then_inc(w_ready, 1)

            def power(k, n, s):
                pool.wait_ge(ln_var[k], 2 * n + s + 1)
                nc.gpsimd.tensor_tensor(rstd[:, k, 2 * s:2 * s + 2], veps[:, k, 2 * s:2 * s + 2],
                                        minus_half[:, 0:2], ALU.pow).then_inc(ln_rstd[k], 1)

            def products(kind, g, q):
                if q < 2:
                    pool.wait_ge(x_read, bank_turn(kind, g, ("ctx", 1)))
                    if q == 0 and kind != "first":
                        pool.wait_ge(mix_ready, 8 * (g - 1) + 6)
                else:
                    use = ("conv", QH * (q - 1) - 1)
                    late = kind == "last" and use in LATE.values()
                    pool.wait_ge(x_written, bank_turn("after", g + 1, use) if late else bank_turn(kind, g, use))
                for i in range(CI):
                    k_i = ctx_T[:, :, q * QH:(q + 1) * QH, :, i:i + 1].rearrange("p c h b i -> p c (h b) i")
                    k_j = ctx_T[:, :, q * QH:(q + 1) * QH, :, i:CI].rearrange("p c h b i -> p c (h b) i")
                    o = kv[:, q % 2, :, :, :, OFF[i]:OFF[i] + CI - i].rearrange("p c h b t -> p c (h b) t")
                    last = nc.gpsimd.tensor_tensor(o, k_i.to_broadcast([P, KC, QH * NB, CI - i]), k_j, ALU.mult)
                last.then_inc(kv_ready, 1)

            def gate(kind, g, b, part):
                if part == 0:
                    pool.wait_ge(x_read, bank_turn(kind, g, ("ln2", b // 2)))
                    if b == 3 and kind != "after":
                        pool.wait_ge(mix_ready, 8 * (g - 1) + 3)
                last = gate_part(nc.gpsimd, kind, b, part)
                if part == 2:
                    last.then_inc(gated_ready[1], 1)

            def add_bias(kind, g, s):
                if s == 0:
                    pool.wait_ge(y_free, 32 * (g - 1) + 16)
                pool.wait_ge(x_read, bank_turn(kind, g, ("back", s)))
                nc.gpsimd.tensor_tensor(y[:, 2 * s:2 * s + 2], x2[:, 2 * s:2 * s + 2],
                                        bias_sb[:, :].rearrange("p (b n) -> p b n", b=1).to_broadcast([P, 2, DM]),
                                        ALU.add).then_inc(y_biased, 1)

            nc.gpsimd.memset(zero[:, :], 0.0)
            nc.gpsimd.memset(one[:, :], 1.0)
            nc.gpsimd.memset(minus_half[:, :], -0.5).then_inc(consts_ready, 1)
            nc.gpsimd.memset(pad_sb[0:CH, 0:P], 0.0).then_inc(pad_zeroed, 1)
            nc.gpsimd.memset(ident[:, :], 0.0).then_inc(consts_ready, 1)
            pool.wait_ge(consts_ready, 2)
            nc.gpsimd.tensor_tensor(zero_r[:, :], zero[:, :], zero[:, :], ALU.add).then_inc(consts_ready, 1)
            nc.gpsimd.tensor_tensor(one_r[:, :], one[:, :], zero[:, :], ALU.add).then_inc(consts_ready, 1)
            nc.gpsimd.affine_select(out=ident[:, :], in_=ident[:, :], compare_op=ALU.not_equal, fill=1.0,
                                    base=0, pattern=[[-1, P]], channel_multiplier=1).then_inc(consts_ready, 1)

            def group(kind, g, last):
                for t in range(2, HEADS + 2):
                    if kind != "first" and t == 5:
                        power(1, g - 1, 0)
                        power(1, g - 1, 1)
                    if t < HEADS and kind != "after":
                        split_head(g, t)
                    if t >= HEADS and not last:
                        split_head(g + 1, t - HEADS)
                    if kind != "first":
                        for q, part in GATE_POOL.get(t, ()):
                            gate(kind, g, q, part)
                        if t == 12:
                            for s in range(2):
                                power(2, g - 1, s)
                                if kind == "after":
                                    add_bias(kind, g, s)
                            if kind != "after":
                                add_bias(kind, g, 0)
                                add_bias(kind, g, 1)
                    if kind != "after":
                        steps = (10, 11, 13, HEADS + 1) if kind == "last" else (10, 11, 13, 14)
                        if t in steps:
                            products(kind, g, steps.index(t))
                    if t == 14 and not last:
                        power(0, g + 1, 0)
                        power(0, g + 1, 1)

            power(0, 0, 0)
            power(0, 0, 1)
            split_head(0, 0)
            split_head(0, 1)
            group("first", 0, False)
            with pool.Fori(1, LAST) as g:
                group("middle", g, False)
            group("last", LAST, True)
            group("after", GROUPS, True)

        @block.scalar
        def _(act):
            def xT_high(g):
                for c in range(KC):
                    act.wait_ge(xT_done, 2 * g + c + 1)
                    after(act, v_done, g * HEADS)
                    nc.scalar.activation(xT_hi[:, c], bank_qk[c][:, :], ACT.Copy).then_inc(xT_hi_ready, 1)

            def save_qk(g, h, m):
                act.wait_ge(qk_done[m], g * HEADS + h + 1)
                after(act, scores_done, g * HEADS + h - 1)
                nc.scalar.activation(qk[:, m, h % 2], bank_qk[m][:, :], ACT.Copy,
                                     scale=(SCALE, 1.0)[m]).then_inc(qk_ready[m], 1)

            def exps(g, h):
                act.wait_ge(max_ready, g * HEADS + h + 1)
                after(act, probs_lo_ready, g * HEADS + h)
                for b in range(NB):
                    last = nc.scalar.activation(probs[:, b], bank_s[:, b * SEQ:(b + 1) * SEQ], ACT.Exp,
                                                bias=neg_max[:, h % 2, b:b + 1], accum_out=row_sum[:, h % 2, b:b + 1])
                last.then_inc(probs_ready, 1)

            def probs_high(g, h):
                act.wait_ge(divided, g * HEADS + h + 1)
                after(act, col_done, g * HEADS + h - 1)
                nc.scalar.activation(probs_hi[:, h % 2], probs[:, :, :], ACT.Copy).then_inc(probs_hi_ready, 1)

            def save_v(g, h):
                act.wait_ge(v_done, g * HEADS + h + 1)
                after(act, vals_lo_ready, g * HEADS + h - VBUF + 1)
                nc.scalar.activation(v_sb[:, h % VBUF], bank_v[:, :], ACT.Copy).then_inc(v_saved, 1)

            def vals_high(g, h):
                act.wait_ge(vals_ready, g * HEADS + h + 1)
                after(act, att_done, g * HEADS + h)
                nc.scalar.activation(vals_hi[:, :], v_sb[:, h % VBUF], ACT.Copy).then_inc(vals_hi_ready, 1)

            def prep_high(p):
                act.wait_ge(prep_loaded[p % 2], 32 * (p // 2 + 1))
                nc.scalar.activation(wv_hi[:, :, 2 * p * HD:(2 * p + 2) * HD], wv_sb[:, p % 2],
                                     ACT.Copy).then_inc(prep_hi_ready, 1)
                nc.scalar.activation(wo_hi[:, 2 * p:2 * p + 2], wo_sb[:, p % 2], ACT.Copy).then_inc(prep_hi_ready, 1)

            def read_bank(kind, g, at):
                what, n = USES[kind].get(at, ("", 0))
                b_h_i = bank_x[:, :].rearrange("p (b h i) -> p b h i", b=NB, h=CH)
                if what == "ctx":
                    after(act, kv_ready, 4 * g)
                    o, i = ctx_T[:, n].rearrange("p h b i -> p b h i"), b_h_i
                elif what == "conv":
                    if n == 0 and kind != "first":
                        for ready in gated_ready:
                            act.wait_ge(ready, 2 * g)
                    o = conv[:, :, n].rearrange("p c b t -> p c (b t)")
                    i = bank_x[:, 0:KC * NB * TRI].rearrange("p (c n) -> p c n", c=KC)
                elif what == "lin_w":
                    o, i = lin_hi[:, :, :].rearrange("p c n -> p (c n)"), bank_x[:, :]
                elif what == "ln2":
                    half = ln2_T[:, :, :, 2 * n:2 * n + 2].rearrange("p c h b i -> p c b h i")
                    half_bank = bank_x[:, :].rearrange("p (c b h i) -> p c b h i", c=KC, b=2, h=CH)
                    act.wait_ge(x_written, bank_turn(kind, g, (what, n)))
                    nc.scalar.activation(half[:, 0], half_bank[:, 0], ACT.Copy)
                    o, i = half[:, 1], half_bank[:, 1]
                elif what == "ln3":
                    o, i = ln3_hi[:, :, 2 * n * P:(2 * n + 2) * P], bank_x[:, :].rearrange("p (c t) -> p c t", c=KC)
                else:
                    return
                if what != "ln2":
                    act.wait_ge(x_written, bank_turn(kind, g, (what, n)))
                if what in ("lin_w", "ln3"):
                    nc.scalar.activation(o, i, ACT.Copy).then_inc(x_hi_ready, 1)
                else:
                    nc.scalar.activation(o, i, ACT.Copy).then_inc(x_read, 1)

            def group(kind, g, last):
                for t in range(HEADS):
                    if kind != "after":
                        save_qk(g, t, 0)
                    read_bank(kind, g, (t, 0))
                    if runs(kind, t - 2):
                        probs_high(g, t - 2)
                    if kind != "after":
                        save_qk(g, t, 1)
                    read_bank(kind, g, (t, 1))
                    read_bank(kind, g, (t, 2))
                    if runs(kind, t - 1):
                        exps(g, t - 1)
                    if t == HEADS - 1 and not last:
                        xT_high(g + 1)
                    if runs(kind, t - 2):
                        vals_high(g, t - 2)
                    if kind != "after":
                        save_v(g, t)
                    if kind == "first" and t % 2 == 0 and t // 2 + 2 < PAIRS:
                        prep_high(t // 2 + 2)
                    read_bank(kind, g, (t, 3))

            xT_high(0)
            prep_high(0)
            prep_high(1)
            group("first", 0, False)
            with act.Fori(1, LAST) as g:
                group("middle", g, False)
            group("last", LAST, True)
            group("after", GROUPS, True)

        @block.vector
        def _(dve):
            def ln_moments(k, n, src, s):
                tiles = range(2 * s, 2 * s + 2)
                for b in tiles:
                    last = nc.vector.bn_stats(stats[:, k, b], src[:, b])
                last.then_inc(ln_stats[k], 1)
                dve.wait_ge(ln_stats[k], 2 * n + s + 1)
                nc.vector.tensor_copy(pace[:, 0:1], stats[:, k, 2 * s, 0:1])
                for b in tiles:
                    last = nc.vector.bn_aggr(mv[:, k, b], stats[:, k, b])
                last.then_inc(ln_mv[k], 1)
                dve.wait_ge(ln_mv[k], 2 * n + s + 1)
                nc.vector.tensor_scalar(veps[:, k, 2 * s:2 * s + 2], mv[:, k, 2 * s:2 * s + 2, 1], EPS, None,
                                        ALU.add).then_inc(ln_var[k], 1)

            def ln_normalise(k, n, src, s):
                dve.wait_ge(ln_rstd[k], 2 * n + s + 1)
                for b in range(2 * s, 2 * s + 2):
                    last = nc.vector.tensor_scalar(ln[:, b], src[:, b], mv[:, k, b, 0:1], rstd[:, k, b:b + 1],
                                                   ALU.subtract, ALU.mult)
                last.then_inc(ln_ready[k], 1)

            def ln1_moments(n, s):
                dve.wait_ge(x_loaded[s], 16 * (n + 1))
                ln_moments(0, n, x_in, s)

            def xT_low(g):
                for c in range(KC):
                    dve.wait_ge(xT_hi_ready, 2 * g + c + 1)
                    nc.vector.tensor_tensor(xT_lo[:, c], bank_qk[c][:, :], xT_hi[:, c].bitcast(F32),
                                            ALU.subtract).then_inc(xT_ready, 1)

            def row_max(g, h):
                dve.wait_ge(scores_done, g * HEADS + h + 1)
                nc.vector.tensor_reduce(out=neg_max[:, h % 2], in_=bank_s[:, :].rearrange("p (b k) -> p b k", b=NB),
                                        op=ALU.max, axis=AX.X, negate=True).then_inc(max_ready, 1)

            def row_inverse(g, h):
                dve.wait_ge(probs_ready, g * HEADS + h + 1)
                nc.vector.reciprocal(row_inv[:, h % 2], row_sum[:, h % 2]).then_inc(inv_ready, 1)

            def divide(g, h):
                dve.wait_ge(inv_ready, g * HEADS + h + 1)
                inv = row_inv[:, h % 2].rearrange("p (b k) -> p b k", k=1).to_broadcast([P, NB, SEQ])
                nc.vector.tensor_tensor(probs[:, :, :], probs[:, :, :], inv, ALU.mult).then_inc(divided, 1)

            def probs_low(g, h):
                dve.wait_ge(probs_hi_ready, g * HEADS + h + 1)
                nc.vector.tensor_tensor(probs_lo[:, h % 2], probs[:, :, :], probs_hi[:, h % 2].bitcast(F32),
                                        ALU.subtract).then_inc(probs_lo_ready, 1)

            def weigh(g, h):
                dve.wait_ge(v_saved, g * HEADS + h + 1)
                dve.wait_ge(col_done, g * HEADS + h + 1)
                v = v_sb[:, h % VBUF]
                nc.vector.tensor_tensor(v, bank_c[:, :], v, ALU.mult).then_inc(vals_ready, 1)

            def vals_low(g, h):
                dve.wait_ge(vals_hi_ready, g * HEADS + h + 1)
                nc.vector.tensor_tensor(vals_lo[:, :], v_sb[:, h % VBUF], vals_hi[:, :].bitcast(F32),
                                        ALU.subtract).then_inc(vals_lo_ready, 1)

            def gate(kind, g, b, part):
                if part == 0:
                    dve.wait_ge(x_read, bank_turn(kind, g, ("ln2", b // 2)))
                    if b == 2:
                        dve.wait_ge(mix_ready, 8 * (g - 1) + (2 if kind == "after" else 4))
                last = gate_part(nc.vector, kind, b, part)
                if part == 2:
                    last.then_inc(gated_ready[0], 1)

            def mix(kind, g, b, c):
                dve.wait_ge(gated_ready[b % 2], 2 * (g - 1) + b // 2 + 1)
                nc.vector.tensor_reduce(out=ln[:, b, c * P:(c + 1) * P].rearrange("p (h j) -> p h j", h=CH),
                                        in_=GATED[kind][b][:, c * CH:(c + 1) * CH], op=ALU.add,
                                        axis=AX.X).then_inc(mix_ready, 1)

            def mixing_piece(kind, g, piece):
                what, b, part = piece
                (gate if what == "gate" else mix)(kind, g, b, part)

            def sum_x2(p, s):
                if s == 0:
                    dve.wait_ge(x2_loaded, 16 * (p + 1))
                    dve.wait_ge(att_done, (p + 1) * HEADS)
                t = x2[:, 2 * s:2 * s + 2].rearrange("p b n -> p (b n)")
                nc.vector.tensor_tensor(t, bank_o[s][:, :], t, ALU.add).then_inc(x2_summed, 1)

            def x2_moments(p, s):
                dve.wait_ge(x2_summed, 2 * p + s + 1)
                ln_moments(1, p, x2, s)

            def x3_moments(kind, g, s):
                dve.wait_ge(x_read, bank_turn(kind, g, ("back", s)))
                ln_moments(2, g - 1, x2, s)

            def read_bank(kind, g, at):
                what, s = USES[kind].get(at, ("", 0))
                if what == "lin_w":
                    dve.wait_ge(x_hi_ready, 1)
                    nc.vector.tensor_tensor(lin_lo[:, :, :].rearrange("p c n -> p (c n)"), bank_x[:, :],
                                            lin_hi[:, :, :].rearrange("p c n -> p (c n)").bitcast(F32),
                                            ALU.subtract).then_inc(x_read, 1)
                if what == "ln3":
                    half = slice(2 * s * P, (2 * s + 2) * P)
                    dve.wait_ge(x_hi_ready, 1 + 2 * (g - 1) + s + 1)
                    nc.vector.tensor_tensor(ln3_lo[:, :, half], bank_x[:, :].rearrange("p (c t) -> p c t", c=KC),
                                            ln3_hi[:, :, half].bitcast(F32), ALU.subtract).then_inc(x_read, 1)
                if what not in ("back", "lin"):
                    return
                if what == "lin":
                    dve.wait_ge(y_biased, 2 * (g - 1) + s + 1)
                dve.wait_ge(x_written, bank_turn(kind, g, (what, s)))
                t = (y if what == "lin" else x2)[:, 2 * s:2 * s + 2].rearrange("p b n -> p (b n)")
                nc.vector.tensor_tensor(t, bank_x[:, :], t, ALU.add).then_inc(x_read, 1)

            def prep_low(p):
                dve.wait_ge(prep_hi_ready, 2 * p + 1)
                hi = wv_hi[:, :, 2 * p * HD:(2 * p + 2) * HD]
                nc.vector.tensor_tensor(wv_lo[:, :, 2 * p * HD:(2 * p + 2) * HD], wv_sb[:, p % 2], hi.bitcast(F32),
                                        ALU.subtract).then_inc(prep_ready, 1)
                dve.wait_ge(prep_hi_ready, 2 * p + 2)
                hi = wo_hi[:, 2 * p:2 * p + 2]
                nc.vector.tensor_tensor(wo_lo[:, 2 * p:2 * p + 2], wo_sb[:, p % 2], hi.bitcast(F32),
                                        ALU.subtract).then_inc(prep_ready, 1)

            def binarise(part):
                if part == 0:
                    dve.wait_ge(lin_loaded, 16)
                    nc.vector.tensor_reduce(out=alpha[:, :], in_=lin_sb, op=ALU.add, axis=AX.X,
                                            apply_absolute_value=True).then_inc(lin_step, 1)
                    nc.vector.tensor_scalar(lin_bin, lin_sb, 0.0, 2.0, ALU.is_ge, ALU.mult).then_inc(lin_step, 1)
                    dve.wait_ge(lin_step, 2)
                    nc.vector.tensor_scalar(alpha[:, :], alpha[:, :], 1.0 / DM, None, ALU.mult).then_inc(lin_step, 1)
                    return
                dve.wait_ge(lin_step, 3)
                for o in range(KC):
                    nc.vector.tensor_scalar(lin_bin[:, o], lin_bin[:, o], -1.0, alpha[:, o:o + 1],
                                            ALU.add, ALU.mult).then_inc(lin_step, 1)
                dve.wait_ge(lin_step, 5)
                nc.vector.tensor_tensor(lin_bin, lin_bin, lin_sb, ALU.subtract).then_inc(lin_step, 1)
                dve.wait_ge(lin_step, 6)
                nc.vector.tensor_tensor(lin_bin, lin_bin, lin_sb, ALU.add).then_inc(lin_ready, 1)

            def group(kind, g, last):
                for t in range(HEADS):
                    if runs(kind, t - 3):
                        vals_low(g, t - 3)
                    if runs(kind, t - 2):
                        row_inverse(g, t - 2)
                        divide(g, t - 2)
                    read_bank(kind, g, (t, 0))
                    if runs(kind, t - 2):
                        probs_low(g, t - 2)
                    if kind != "first" and t == 3:
                        x2_moments(g - 1, 1)
                    if kind != "first" and t == 4:
                        ln_normalise(1, g - 1, x2, 0)
                        ln_normalise(1, g - 1, x2, 1)
                    for piece in MIX_EARLY.get(t, ()) if kind != "first" else ():
                        mixing_piece(kind, g, piece)
                    read_bank(kind, g, (t, 1))
                    if not last and t in (13, 14):
                        ln1_moments(g + 1, t - 13)
                    read_bank(kind, g, (t, 2))
                    if runs(kind, t - 1):
                        row_max(g, t - 1)
                    if t == HEADS - 1 and not last:
                        xT_low(g + 1)
                    if runs(kind, t - 2):
                        weigh(g, t - 2)
                    if kind != "first" and t == 2:
                        sum_x2(g - 1, 0)
                        sum_x2(g - 1, 1)
                        x2_moments(g - 1, 0)
                    if kind != "first" and t == 11:
                        x3_moments(kind, g, 0)
                    if kind != "first" and t == 12:
                        ln_normalise(2, g - 1, x2, 0)
                        ln_normalise(2, g - 1, x2, 1)
                    read_bank(kind, g, (t, 3))
                    if kind == "first":
                        if t % 2 == 1 and t // 2 + 2 < PAIRS:
                            prep_low(t // 2 + 2)
                        if t in (2, 4):
                            binarise(t // 2 - 1)
                    else:
                        for piece in MIX_LATE.get(t, ()):
                            mixing_piece(kind, g, piece)
                        if t == 11:
                            x3_moments(kind, g, 1)
                    if not last:
                        if t == 14:
                            if kind != "first":
                                dve.wait_ge(x_written, bank_turn(kind, g, ("ln3", 1)))
                            ln_normalise(0, g + 1, x_in, 0)
                            ln_normalise(0, g + 1, x_in, 1)

            def finish(g):
                for h in (-2, -1):
                    vals_low(g, h - 1)
                    row_inverse(g, h)
                    divide(g, h)
                    probs_low(g, h)
                    if h == -2:
                        row_max(g, -1)
                    weigh(g, h)
                vals_low(g, -1)
                for s in range(2):
                    sum_x2(g - 1, s)
                    x2_moments(g - 1, s)
                ln_normalise(1, g - 1, x2, 0)
                ln_normalise(1, g - 1, x2, 1)
                for piece in [("gate", 0, 0), ("gate", 0, 1), ("gate", 0, 2), ("mix", 0, 0), ("mix", 0, 1),
                              ("gate", 2, 0), ("gate", 2, 1), ("gate", 2, 2), ("mix", 2, 0), ("mix", 2, 1)]:
                    mixing_piece("after", g, piece)
                read_bank("after", g, (10, 0))
                x3_moments("after", g, 0)
                ln_normalise(2, g - 1, x2, 0)
                read_bank("after", g, (10, 1))
                x3_moments("after", g, 1)
                read_bank("after", g, (11, 0))
                ln_normalise(2, g - 1, x2, 1)
                for at in ((11, 1), (12, 0), (12, 1)):
                    read_bank("after", g, at)

            ln1_moments(0, 0)
            ln1_moments(0, 1)
            ln_normalise(0, 0, x_in, 0)
            ln_normalise(0, 0, x_in, 1)
            xT_low(0)
            prep_low(0)
            prep_low(1)
            dve.wait_ge(ssm_loaded, 32)
            dve.wait_ge(pad_zeroed, 1)
            nc.vector.tensor_tensor(pad_sb[0:CH, P:P + 1], pad_sb[0:CH, P:P + 1], skip_sb[0:CH, :],
                                    ALU.add).then_inc(pad_ready, 1)
            group("first", 0, False)
            with dve.Fori(1, LAST) as g:
                group("middle", g, False)
            group("last", LAST, True)
            finish(GROUPS)

        @block.tensor
        def _(pe):
            def three(out_, a_hi, a_lo, b_hi, b_lo, start, stop):
                nc.tensor.matmul(out_, a_hi, b_hi, start=start, stop=False)
                nc.tensor.matmul(out_, a_hi, b_lo, start=False, stop=False)
                return nc.tensor.matmul(out_, a_lo, b_hi, start=False, stop=stop)

            def transpose_chunk(o, src, c, tiles=range(NB)):
                for b in tiles:
                    last = nc.tensor.transpose(o[:, b * P:(b + 1) * P], src[:, b, c * P:(c + 1) * P], ident[:, :])
                return last

            def transpose_half(s):
                for c in range(KC):
                    for b in range(2):
                        last = nc.tensor.transpose(bank_x[:, (2 * c + b) * P:(2 * c + b + 1) * P],
                                                   ln[:, 2 * s + b, c * P:(c + 1) * P], ident[:, :])
                return last

            def project_qk(g, h, m):
                if m == 0:
                    pe.wait_ge(w_ready, g * HEADS + h + 1)
                after(pe, qk_ready[m], g * HEADS + h)
                for c in range(KC):
                    if h == 0 and m == 0:
                        pe.wait_ge(xT_ready, 2 * g + c + 1)
                    last = three(bank_qk[m][:, :], w_hi[:, h % 2, m, c], w_lo[:, h % 2, m, c],
                                 xT_hi[:, c], xT_lo[:, c], c == 0, c == KC - 1)
                last.then_inc(qk_done[m], 1)

            def project_v(kind, g, h):
                if kind == "first":
                    pe.wait_ge(prep_ready, 2 * (h // 2) + 1)
                after(pe, v_saved, g * HEADS + h)
                s = slice(h * HD, (h + 1) * HD)
                for c in range(KC):
                    last = three(bank_v[:, :], wv_hi[:, c, s], wv_lo[:, c, s], xT_hi[:, c], xT_lo[:, c],
                                 c == 0, c == KC - 1)
                last.then_inc(v_done, 1)

            def scores(g, h):
                pe.wait_ge(qk_ready[0], g * HEADS + h + 1)
                pe.wait_ge(qk_ready[1], g * HEADS + h + 1)
                after(pe, probs_ready, g * HEADS + h)
                r = h % 2
                for b in range(NB):
                    s = slice(b * SEQ, (b + 1) * SEQ)
                    last = nc.tensor.matmul(bank_s[:, s], qk[:, 0, r, s], qk[:, 1, r, s], start=True, stop=True)
                last.then_inc(scores_done, 1)

            def column_sums(g, h):
                pe.wait_ge(probs_lo_ready, g * HEADS + h + 1)
                after(pe, vals_ready, g * HEADS + h)
                ones = one_r[:, :].to_broadcast([P, P])
                nc.tensor.matmul(bank_c[:, :], ones, probs_hi[:, h % 2].rearrange("p b k -> p (b k)"), start=True,
                                 stop=False)
                nc.tensor.matmul(bank_c[:, :], ones, probs_lo[:, h % 2].rearrange("p b k -> p (b k)"), start=False,
                                 stop=True).then_inc(col_done, 1)

            def output_product(kind, g, h):
                n = g * HEADS + h
                h = h % HEADS
                if kind == "first":
                    pe.wait_ge(prep_ready, 2 * (h // 2) + 2)
                if h == 0:
                    after(pe, x2_summed, 2 * g)
                    for o in bank_o:
                        nc.tensor.matmul(o[:, :], zero_r[:, :].to_broadcast([P, P]),
                                         zero_r[:, :].to_broadcast([P, 2 * DM]), start=True, stop=False)
                pe.wait_ge(vals_lo_ready, n + 1)
                for b in range(NB):
                    s = slice(b * P, (b + 1) * P)
                    last = three(bank_o[b // 2][:, (b % 2) * DM:(b % 2 + 1) * DM], vals_hi[:, s], vals_lo[:, s],
                                 wo_hi[:, h], wo_lo[:, h], False, h == HEADS - 1 and b % 2 == 1)
                last.then_inc(att_done, 1)

            def transpose_next_x(g):
                for s in range(2):
                    pe.wait_ge(ln_ready[0], 2 * g + s + 1)
                    for c in range(KC):
                        if s == 0:
                            after(pe, qk_ready[c], g * HEADS)
                        last = transpose_chunk(bank_qk[c], ln, c, range(2 * s, 2 * s + 2))
                        if s == 1:
                            last.then_inc(xT_done, 1)

            def back_to_tokens(tiles):
                for b in tiles:
                    for c in range(KC):
                        last = nc.tensor.transpose(bank_x[:, (b % 2) * DM + c * P:(b % 2) * DM + (c + 1) * P],
                                                   ln[:, b, c * P:(c + 1) * P], ident[:, :])
                return last

            def back_and_sum(g, s):
                pe.wait_ge(mix_ready, 8 * (g - 1) + 2 * (s + 1))
                back_to_tokens([2 * s])
                pe.wait_ge(gated_ready[1], 2 * (g - 1) + s + 1)
                products = GATED["after"][2 * s + 1].rearrange("p n j i -> p (n j) i")
                for c in range(KC):
                    for i in range(CI):
                        last = nc.tensor.matmul(bank_x[:, DM + c * P:DM + (c + 1) * P],
                                                products[:, c * P:(c + 1) * P, i], ident[:, :],
                                                start=i == 0, stop=i == CI - 1)
                return last

            def convolve(g, h):
                if h % QH == 0:
                    pe.wait_ge(kv_ready, 4 * g + h // QH + 1)
                src = kv[:, (h // QH) % 2, :, h % QH].rearrange("p c b t -> p c (b t)")
                n = NB * TRI
                near, far = toeplitz[:, h, 0:P], toeplitz[:, h, P:2 * P]
                nc.tensor.matmul(bank_x[:, 0:n], near, src[:, 0], start=True, stop=True)
                nc.tensor.matmul(bank_x[:, n:2 * n], near, src[:, 1], start=True, stop=False)
                return nc.tensor.matmul(bank_x[:, n:2 * n], far, src[:, 0], start=False, stop=True)

            def linear(s):
                for b in range(2 * s, 2 * s + 2):
                    for c in range(KC):
                        t = slice(b * P, (b + 1) * P)
                        last = three(bank_x[:, (b % 2) * DM:(b % 2 + 1) * DM], ln3_hi[:, c, t], ln3_lo[:, c, t],
                                     lin_hi[:, c], lin_lo[:, c], c == 0, c == KC - 1)
                return last

            def transpose_lin():
                pe.wait_ge(lin_ready, 1)
                for c in range(KC):
                    for o in range(KC):
                        last = nc.tensor.transpose(bank_x[:, (2 * c + o) * P:(2 * c + o + 1) * P],
                                                   lin_bin[:, o, c * P:(c + 1) * P], ident[:, :])
                return last

            def write_bank(kind, g, at):
                if at not in USES[kind]:
                    return
                what, n = USES[kind][at]
                after(pe, x_read, bank_turn(kind, g, (what, n)) - 1)
                if what == "ln2":
                    pe.wait_ge(ln_ready[1], 2 * (g - 1) + n + 1)
                    last = transpose_half(n)
                elif what == "ctx":
                    pe.wait_ge(ctx_loaded, 16 * g + 16)
                    last = transpose_chunk(bank_x, ctx_sb, n)
                elif what == "back":
                    if kind == "after":
                        last = back_and_sum(g, n)
                    else:
                        pe.wait_ge(mix_ready, 8 * g)
                        last = back_to_tokens(range(2 * n, 2 * n + 2))
                elif what == "ln3":
                    pe.wait_ge(ln_ready[2], 2 * (g - 1) + n + 1)
                    last = transpose_half(n)
                elif what == "lin":
                    last = linear(n)
                elif what == "conv":
                    if kind == "first" and n == 0:
                        pe.wait_ge(toeplitz_loaded, 16)
                    last = convolve(g - 1 if kind == "after" else g, n)
                else:
                    last = transpose_lin()
                last.then_inc(x_written, 1)

            def group(kind, g, last):
                for t in range(HEADS):
                    if kind != "after":
                        project_qk(g, t, 0)
                    write_bank(kind, g, (t, 0))
                    if kind != "after":
                        project_qk(g, t, 1)
                    if runs(kind, t - 1) and kind == "after":
                        scores(g, t - 1)
                    write_bank(kind, g, (t, 1))
                    changing = t == HEADS - 1 and not last
                    if runs(kind, t - 3) and not changing:
                        output_product(kind, g, t - 3)
                    if not changing:
                        write_bank(kind, g, (t, 2))
                    if runs(kind, t - 1) and kind != "after":
                        scores(g, t - 1)
                    if changing:
                        transpose_next_x(g + 1)
                        write_bank(kind, g, (t, 2))
                    if runs(kind, t - 2) and not changing:
                        column_sums(g, t - 2)
                    if kind != "after":
                        project_v(kind, g, t)
                    if changing:
                        output_product(kind, g, t - 3)
                        column_sums(g, t - 2)
                    write_bank(kind, g, (t, 3))

            pe.wait_ge(consts_ready, 5)
            transpose_next_x(0)
            group("first", 0, False)
            with pe.Fori(1, LAST) as g:
                group("middle", g, False)
            group("last", LAST, True)
            group("after", GROUPS, True)


_INS = ["x", "ctx_2048", "L0_attn_w_qkv", "L0_attn_w_o", "L0_xattn_ssm_kernel", "L0_xattn_D", "L0_ffn_weight",
        "L0_ffn_bias"]


def kernel(**inputs):
    import numpy as _np
    import concourse.bacc as _bacc
    from concourse import mybir as _mybir
    from concourse.bass_utils import run_bass_kernel_spmd as _run

    nc = _bacc.Bacc("TRN2", target_bir_lowering=False, num_devices=1)
    arrays, args = {}, []
    for name in _INS:
        a = _np.ascontiguousarray(inputs[name])
        arrays[f"in_{name}"] = a
        args.append(nc.dram_tensor(f"in_{name}", a.shape, _mybir.dt.from_np(a.dtype), kind="ExternalInput").ap())
    args.append(nc.dram_tensor("out_0", inputs["x"].shape, _mybir.dt.float32, kind="ExternalOutput").ap())
    decoder_layer(nc, *args)
    r = _run(nc, [arrays], core_ids=[0])
    return r.results[0]["out_0"]
```
